# Optimizing a Trainium2 kernel written in Bass

```python
import numpy as np
import jax
import jax.numpy as jnp

def _softmax(x, axis=-1):
    return jax.nn.softmax(x, axis=axis)
def _gelu(x):
    return jax.nn.gelu(x, approximate=True)
def _silu(x):
    return jax.nn.silu(x)
def _sigmoid(x):
    return jax.nn.sigmoid(x)
def _layernorm(x, axis=-1, eps=1e-5):
    m = jnp.mean(x, axis=axis, keepdims=True)
    v = jnp.var(x, axis=axis, keepdims=True)
    return (x - m) / jnp.sqrt(v + eps)
def _scatter_add(tgt, idx, src, axis=0):
    return tgt.at[idx].add(src)
def _segment_sum(src, seg, n):
    return jax.ops.segment_sum(src, seg, n)

kernel_name = 'mk_adj_preln_d2_adj_64_445e79'

def setup_inputs(seed: int = 0):
    np.random.seed(seed)
    _w = jnp.asarray
    def _rec_inputs():
        import jax
        import jax.numpy as jnp
        _gk = jax.random.key(seed)
        x = -0.006082 + 1.001 * jax.random.normal(jax.random.fold_in(_gk, 1), (8192, 64), jnp.float32)
        _w = (1.0 + jnp.arange(8192, dtype=jnp.float32)) ** -0.5
        _w = _w / _w.mean()
        _pij = jnp.clip(0.000488281 * _w[:, None] * _w[None, :], 0.0, 1.0)
        _a = jax.random.uniform(jax.random.fold_in(_gk, 2), (8192, 8192)) < _pij
        adj = _a.astype(jnp.int32)
        return x, adj
    x, adj = _rec_inputs()
    def _L0_gnn_setup():
        import jax, jax.numpy as jnp
        import numpy as np
        ALPHA = 0.2
        NEG_INF = -9000000000000000.0
        key = jax.random.key(seed)
        k1, k2, k3, k4 = jax.random.split(key, 4)
        N, F_IN, F_OUT = (1024, 64, 64)
        h = jax.random.normal(k1, (N, F_IN), dtype=jnp.float32)
        adj = jax.random.randint(k2, (N, N), 0, 2, dtype=jnp.int32)
        lim_W = 1.414 * np.sqrt(6.0 / (F_IN + F_OUT))
        W = jax.random.uniform(k3, (F_IN, F_OUT), minval=-lim_W, maxval=lim_W, dtype=jnp.float32)
        lim_a = 1.414 * np.sqrt(6.0 / (2 * F_OUT + 1))
        a = jax.random.uniform(k4, (2 * F_OUT, 1), minval=-lim_a, maxval=lim_a, dtype=jnp.float32)
        return {'h': h, 'adj': adj, 'W': W, 'a': a}
    _L0_gnn_all = _L0_gnn_setup()
    _L0_gnn_in = {k: v for k, v in _L0_gnn_all.items() if k in ('W', 'a', )}
    del _L0_gnn_all

    def _L1_gnn_setup():
        import jax, jax.numpy as jnp
        import numpy as np
        N = 8192
        F_IN = 64
        F_OUT = 64
        NEG_SLOPE = 0.01
        MASK_FILL = -1000000000000.0
        key = jax.random.key(seed)
        k1, k2, k3, k4 = jax.random.split(key, 4)
        x = jax.random.normal(k1, (N, F_IN), dtype=jnp.float32)
        adj_matrix = jax.random.randint(k2, (N, N), 0, 2, dtype=jnp.int32)
        W = jax.random.normal(k3, (F_IN, F_OUT), dtype=jnp.float32) * (1.0 / np.sqrt(F_IN))
        a = jax.random.normal(k4, (2 * F_IN, 1), dtype=jnp.float32) * (1.0 / np.sqrt(2 * F_IN))
        return {'x': x, 'adj_matrix': adj_matrix, 'W': W, 'a': a}
    _L1_gnn_all = _L1_gnn_setup()
    _L1_gnn_in = {k: v for k, v in _L1_gnn_all.items() if k in ('W', 'a', )}
    del _L1_gnn_all

    return {
        "x": x,
        "adj": adj,
        "L0_gnn_W": _L0_gnn_in["W"],
        "L0_gnn_a": _L0_gnn_in["a"],
        "L1_gnn_W": _L1_gnn_in["W"],
        "L1_gnn_a": _L1_gnn_in["a"],
    }

def reference(x, adj, L0_gnn_W, L0_gnn_a, L1_gnn_W, L1_gnn_a):
    import jax
    import jax.numpy as jnp
    def _L0_gnn_ref(h, adj, W, a):
        import jax, jax.numpy as jnp
        import numpy as np
        ALPHA = 0.2
        NEG_INF = -9000000000000000.0
        F_OUT = W.shape[1]
        Wh = h @ W
        a1, a2 = (a[:F_OUT, 0], a[F_OUT:, 0])
        e = (Wh @ a1)[:, None] + (Wh @ a2)[None, :]
        e = jax.nn.leaky_relu(e, negative_slope=ALPHA)
        scores = jnp.where(adj > 0, e, jnp.float32(NEG_INF))
        attention = jax.nn.softmax(scores, axis=1)
        h_prime = attention @ Wh
        return jax.nn.elu(h_prime)

    def _L1_gnn_ref(x, adj_matrix, W, a):
        import jax, jax.numpy as jnp
        import numpy as np
        N = 8192
        F_IN = 64
        F_OUT = 64
        NEG_SLOPE = 0.01
        MASK_FILL = -1000000000000.0
        h = x @ W
        a1 = a[:F_OUT, 0]
        a2 = a[F_OUT:, 0]
        f1 = h @ a1
        f2 = h @ a2
        e = jax.nn.leaky_relu(f1[:, None] + f2[None, :], NEG_SLOPE)
        e = jnp.where(adj_matrix > 0, e, MASK_FILL)
        attention = jax.nn.softmax(e, axis=1)
        h_prime = attention @ h
        return jax.nn.elu(h_prime)

    h = jnp.maximum(_layernorm(x, axis=-1), 0.0)
    x = x + _L0_gnn_ref(h, adj, L0_gnn_W, L0_gnn_a)
    h = jnp.maximum(_layernorm(x, axis=-1), 0.0)
    x = x + _L1_gnn_ref(h, adj, L1_gnn_W, L1_gnn_a)
    return x


_drawn_inputs = setup_inputs


def setup_inputs(seed=0):
    import zlib

    import numpy as np

    out = dict(_drawn_inputs(seed))
    spreads = {}
    factors = {}
    for name, (base, spread) in spreads.items():
        noise = np.random.default_rng([zlib.crc32(name.encode()), seed]).standard_normal(out[name].shape)
        drawn = base * np.exp(spread * noise) if base else spread * noise
        out[name] = jnp.asarray(drawn.astype(out[name].dtype))
    for name, factor in factors.items():
        out[name] = (out[name] * factor).astype(out[name].dtype)
    return out
```

```python
from contextlib import ExitStack

import numpy as np

import concourse.bass as bass
from concourse import mybir


P = 128
BITS = 16
WORDS = P // BITS
CHUNK_BLOCKS = 8
CHUNK = CHUNK_BLOCKS * P
ADJ_SLOTS = 8
EARLY_SLOTS = 4
MASK_SLOTS = 4
SIGN_SLOTS = 2
EPS = 1e-5
SHIFT = 32.0
TINY = 2.0 ** -61
NEAR_ZERO = 2.0 ** -60
TWO_TWICE = 0x4040

ALU = mybir.AluOpType
ACT = mybir.ActivationFunctionType
AX = mybir.AxisListType
BF16 = mybir.dt.bfloat16
FP8 = mybir.dt.float8e4
F32 = mybir.dt.float32
I32 = mybir.dt.int32
U16 = mybir.dt.uint16
U32 = mybir.dt.uint32


def two_layer_graph_attention(nc, x, adj, W0, a0, W1, a1, identity_in, powers_in, out):
    N, F = x.shape
    TILES = N // P
    BLOCKS = N // P
    CHUNKS = N // CHUNK
    HALF_CHUNKS = CHUNKS // 2
    HALF_BLOCKS = BLOCKS // 2
    MAIN_PER_CHUNK = BLOCKS // HALF_CHUNKS
    TW = BLOCKS * WORDS
    HW = TW // 2
    C1 = F + 1
    COLS = 3 * C1
    GROUP = 4
    GROUPS = BLOCKS // GROUP
    LAYERS = ((W0, a0, 0.2), (W1, a1, 0.01))

    x1 = nc.dram_tensor("x_after_layer0", (N, F), F32).ap()
    threshold_dram = [nc.dram_tensor(f"threshold{l}", (BLOCKS, P), F32).ap() for l in range(2)]

    with ExitStack() as ctx:
        def sb(name, shape, dt):
            return ctx.enter_context(nc.sbuf_tensor(name, shape, dt))

        def ps(name, shape, dt=F32):
            return ctx.enter_context(nc.psum_tensor(name, shape, dt))

        def sem(name):
            return ctx.enter_context(nc.semaphore(name))

        packed = sb("packed_adj", [P, TILES * TW], U16)
        values = sb("values", [P, 2, BLOCKS, 3, C1], BF16)
        thresholds = sb("thresholds", [P, N], F32)
        work = sb("work", [P, 2, BLOCKS, P], FP8)
        adj_in = sb("adj_in", [P, ADJ_SLOTS, CHUNK], I32)
        mask = sb("mask", [P, MASK_SLOTS, CHUNK], FP8)
        sign = sb("sign", [P, SIGN_SLOTS, CHUNK], BF16)
        sign_words = sb("sign_words", [P, TW], U16)
        steep_words = sb("steep_words", [P, TW], U16)
        shallow_words = sign_words
        identity = sb("identity", [P, P], F32)
        powers_f = sb("powers_f", [P, WORDS], F32)
        powers = sb("powers", [P, WORDS], BF16)
        s_row = sb("s_row", [P, TILES], F32)
        scale_a = sb("scale_a", [P, TILES], F32)
        scale_c = sb("scale_c", [P, TILES], F32)
        mean_wh = sb("mean_wh", [P, F], F32)
        sums = sb("sums", [P, 2, COLS], F32)
        total = sb("total", [P, C1], F32)
        e_small = sb("e_small", [P, 4], F32)
        e_mid = sb("e_mid", [P, 3, F], F32)
        x_in = sb("x_in", [P, F], F32)
        x_out = sb("x_out", [P, F], F32)
        xs = work[:].rearrange("p a b c -> p (a b c)").bitcast(F32).rearrange("p (b f) -> p b f", b=BLOCKS)
        hs = adj_in[:, EARLY_SLOTS:, :].rearrange("p a b -> p (a b)").bitcast(F32).rearrange("p (b f) -> p b f", b=BLOCKS)
        hT = sign[:].rearrange("p a b -> p (a b)").bitcast(F32).rearrange("p (s c) -> p s c", c=P)
        small = mask[:].rearrange("p a b -> p (a b)").bitcast(F32)
        cols = small[:, 0:8 * BLOCKS].rearrange("p (a b) -> p a b", a=8)
        sd = small[:, 8 * BLOCKS:10 * BLOCKS].rearrange("p (b t) -> p b t", t=2)
        wT = small[0:F, 10 * BLOCKS:10 * BLOCKS + P]
        dT = small[0:BLOCKS, 10 * BLOCKS + P:10 * BLOCKS + 2 * P]
        spare = sums[:].rearrange("p a b -> p (a b)")
        ones = spare[:, 0:P]
        wpair = spare[:, P:P + 2 * (F + 2)].rearrange("p (a b) -> p a b", a=2)
        w_twice = spare[:, P + 2 * (F + 2):P + 2 * (F + 2) + F]
        a_cols = sb("a_cols", [F, 2], F32)
        one_col = sb("one_col", [P, 4], F32)

        acc = [ps("acc_steep", [P, 512]), ps("acc_shallow", [P, 512])]
        pack = [ps(f"pack{h}", [P, 2, HW]) for h in range(2)]
        turn = [ps(f"turn{h}", [P, 512]) for h in range(2)]
        feat = [ps(f"feat{h}", [P, 512]) for h in range(2)]

        consts_in = sem("consts_in")
        params_in = sem("params_in")
        adj_loaded = [sem(f"adj_loaded{i}") for i in range(ADJ_SLOTS)]
        x_loaded = sem("x_loaded")
        thr_stored = sem("thr_stored")
        thr_loaded = sem("thr_loaded")
        step = sem("dve_step")
        params_free = sem("params_free")
        w_ready = sem("w_ready")
        wt_done = sem("wt_done")
        wt_ready = sem("wt_ready")
        wa_done = sem("wa_done")
        wpair_ready = sem("wpair_ready")
        var_ready = sem("var_ready")
        std_ready = sem("std_ready")
        h_ready = sem("h_ready")
        turned = sem("turned")
        hT_ready = sem("hT_ready")
        feat_done = sem("feat_done")
        feat_read = sem("feat_read")
        mean_done = sem("mean_done")
        dmax_ready = sem("dmax_ready")
        dmax_turned = sem("dmax_turned")
        top_ready = sem("top_ready")
        top_spread = sem("top_spread")
        exp_args = sem("exp_args")
        factors_ready = sem("factors_ready")
        thr_ready = sem("thr_ready")
        thr_turned = sem("thr_turned")
        dT_ready = sem("dT_ready")
        values_ready = sem("values_ready")
        mask_ready = sem("mask_ready")
        sign_ready = sem("sign_ready")
        chunk_packed = sem("chunk_packed")
        words_read = sem("words_read")
        split_step = sem("split_step")
        mat_ready = [sem("steep_ready"), sem("shallow_ready")]
        mat_used = [sem("steep_used"), sem("shallow_used")]
        sums_ready = [sem("steep_sums"), sem("shallow_sums")]
        sums_used = sem("sums_used")
        epi = sem("epilogue_step")
        neg_ready = sem("neg_ready")
        exp_ready = sem("exp_ready")
        out_ready = sem("out_ready")
        x_in_loaded = sem("x_in_loaded")
        out_stored = sem("out_stored")

        EPI_STEPS = 7
        block = ctx.enter_context(nc.Block())

        @block.sync
        def _(sp):
            sp.dma_start(identity[:], identity_in).then_inc(consts_in, 16)
            sp.dma_start(powers_f[:], powers_in).then_inc(consts_in, 16)

            def load_adj(k):
                for c in range(CHUNKS):
                    sp.wait_ge(mask_ready, CHUNKS * k + (c - ADJ_SLOTS + 1))
                    sp.dma_start(adj_in[:, c % ADJ_SLOTS, :],
                                 adj[bass.ds(k * P, P), c * CHUNK:(c + 1) * CHUNK]
                                 ).then_inc(adj_loaded[c % ADJ_SLOTS], 16)

            for l, (W, a, _) in enumerate(LAYERS):
                sp.wait_ge(params_free, l + 1)
                for h in range(2):
                    sp.dma_start(w_twice[h * F:(h + 1) * F, :], W).then_inc(params_in, 16)
                    sp.dma_start(wpair[h * F:(h + 1) * F, h, 0:F], W).then_inc(params_in, 16)
                sp.dma_start(a_cols[:], a.rearrange("(t o) u -> o (t u)", t=2),
                             allow_slow_non_contiguous=True).then_inc(params_in, 16)
                if l == 1:
                    sp.wait_ge(out_stored, 16 * TILES)
                    sp.wait_ge(mat_used[0], TILES)
                    sp.wait_ge(mat_used[1], TILES)
                src = x if l == 0 else x1
                sp.dma_start(xs, src.rearrange("(b p) f -> p b f", p=P)).then_inc(x_loaded, 16)
                if l == 0:
                    for c in range(EARLY_SLOTS):
                        sp.dma_start(adj_in[:, c, :], adj[0:P, c * CHUNK:(c + 1) * CHUNK]
                                     ).then_inc(adj_loaded[c], 16)
                sp.wait_ge(dT_ready, l + 1)
                sp.dma_start(threshold_dram[l], dT).then_inc(thr_stored, 16)
                sp.wait_ge(thr_stored, 16 * (l + 1))
                if l == 1:
                    sp.wait_ge(sign_ready, CHUNKS * TILES)
                sp.dma_start(thresholds[:], threshold_dram[l].rearrange("b p -> (b p)").partition_broadcast(P)
                             ).then_inc(thr_loaded, 16)
                if l == 0:
                    sp.wait_ge(values_ready, 1)
                    for c in range(EARLY_SLOTS, CHUNKS):
                        sp.dma_start(adj_in[:, c % ADJ_SLOTS, :], adj[0:P, c * CHUNK:(c + 1) * CHUNK]
                                     ).then_inc(adj_loaded[c % ADJ_SLOTS], 16)
                    with sp.Fori(1, TILES) as k:
                        load_adj(k)

        @block.gpsimd
        def _(pool):
            for l in range(2):
                src = x if l == 0 else x1
                dst = x1 if l == 0 else out

                def rows(k, first=False):
                    if not first:
                        pool.wait_ge(out_ready, l * TILES + k)
                    pool.nop(nofuse=True)
                    pool.dma_start(x_in[:], src[bass.ds(k * P, P), :]).then_inc(x_in_loaded, 16)
                    pool.wait_ge(out_ready, l * TILES + k + 1)
                    pool.nop(nofuse=True)
                    pool.dma_start(dst[bass.ds(k * P, P), :], x_out[:]).then_inc(out_stored, 16)

                if l == 1:
                    pool.wait_ge(out_stored, 16 * TILES)
                rows(0, first=(l == 0))
                with pool.Fori(1, TILES) as k:
                    rows(k)
            pool.wait_ge(out_stored, 16 * 2 * TILES)

        @block.scalar
        def _(act):
            for l, (_, _, slope) in enumerate(LAYERS):
                act.wait_ge(var_ready, l + 1)
                nc.scalar.activation(cols[:, 1, :], cols[:, 0, :], ACT.Sqrt).then_inc(std_ready, 1)
                for g in range(GROUPS):
                    act.wait_ge(turned, GROUPS * l + g + 1)
                    if g >= 2:
                        act.wait_ge(feat_done, GROUPS * l + g - 1)
                    nc.scalar.copy(hT[:, 2 * (g % 2):2 * (g % 2) + 2, :].rearrange("p a b -> p (a b)")
                                   , turn[g % 2][:, 0:2 * P]).then_inc(hT_ready, 1)
                act.wait_ge(exp_args, l + 1)
                d = sd[:, :, 1]
                nc.scalar.activation(cols[:, 2, :], d, ACT.Exp, bias=one_col[:, 1:2], scale=1.0)
                nc.scalar.activation(cols[:, 3, :], d, ACT.Exp, bias=one_col[:, 2:3], scale=slope)
                nc.scalar.activation(scale_a[:], cols[:, 4, :], ACT.Exp)
                nc.scalar.activation(scale_c[:], cols[:, 5, :], ACT.Exp).then_inc(factors_ready, 1)
                act.wait_ge(factors_ready, l + 1)
                act.wait_ge(thr_loaded, 16 * (l + 1))
                act.wait_ge(values_ready, l + 1)

                def signs(k, c):
                    n = l * TILES * CHUNKS + k * CHUNKS + c
                    if not (l == 0 and isinstance(k, int) and n < SIGN_SLOTS):
                        act.wait_ge(chunk_packed, n - (SIGN_SLOTS - 1))
                    act.nop(nofuse=True)
                    nc.scalar.activation(sign[:, c % SIGN_SLOTS, :], thresholds[:, c * CHUNK:(c + 1) * CHUNK],
                                         ACT.Sign, bias=s_row[:, bass.ds(k, 1)]).then_inc(sign_ready, 1)

                def scaled_sums(k, w):
                    n = l * TILES + k
                    act.wait_ge(mat_used[w], n + 1)
                    if not (l == 0 and isinstance(k, int) and k == 0):
                        act.wait_ge(sums_used, n)
                    act.nop(nofuse=True)
                    nc.scalar.activation(sums[:, w, :], acc[w][:, 0:COLS], ACT.Copy,
                                         scale=(scale_a, scale_c)[w][:, bass.ds(k, 1)]
                                         ).then_inc(sums_ready[w], 1)

                def negative_exp(k):
                    act.wait_ge(neg_ready, l * TILES + k + 1)
                    nc.scalar.activation(e_mid[:, 2, :], e_mid[:, 1, :], ACT.Exp).then_inc(exp_ready, 1)

                def tile(k, first=False, next1=True, next2=True):
                    if not first:
                        scaled_sums(k - 1, 1)
                    for c in range(HALF_CHUNKS, CHUNKS):
                        if next1:
                            signs(k + 1, c)
                        if c == CHUNKS - 2 and not first:
                            negative_exp(k - 1)
                    if next2:
                        signs(k + 2, 0)
                        signs(k + 2, 1)
                    scaled_sums(k, 0)
                    if next2:
                        for c in range(2, HALF_CHUNKS):
                            signs(k + 2, c)

                for c in range(CHUNKS):
                    signs(0, c)
                for c in range(HALF_CHUNKS):
                    signs(1, c)
                tile(0, first=True)
                with act.Fori(1, TILES - 2) as k:
                    tile(k)
                tile(TILES - 2, next2=False)
                tile(TILES - 1, next1=False, next2=False)
                scaled_sums(TILES - 1, 1)
                negative_exp(TILES - 1)

        @block.tensor
        def _(pe):
            pe.wait_ge(consts_in, 32)
            for l in range(2):
                pe.wait_ge(w_ready, l + 1)
                pe.transpose(acc[0][0:F, 0:P], w_twice, identity[:]).then_inc(wt_done, 1)
                pe.wait_ge(wt_ready, l + 1)
                pe.matmul(acc[1][:, 0:2], wT, a_cols[:], start=True, stop=True).then_inc(wa_done, 1)
                pe.wait_ge(wpair_ready, l + 1)
                pe.wait_ge(h_ready, l + 1)

                def turn_group(g):
                    if g >= 2:
                        pe.wait_ge(hT_ready, GROUPS * l + g - 1)
                    for q in range(2):
                        b = GROUP * g + 2 * q
                        mm = pe.transpose(turn[g % 2][:, q * P:(q + 1) * P],
                                          hs[:, b:b + 2, :].rearrange("p b f -> p (b f)"), identity[:])
                    mm.then_inc(turned, 1)

                turn_group(0)
                for g in range(GROUPS):
                    if g + 1 < GROUPS:
                        turn_group(g + 1)
                    pe.wait_ge(hT_ready, GROUPS * l + g + 1)
                    if g >= 2:
                        pe.wait_ge(feat_read, GROUPS * l + g - 1)
                    for q in range(2):
                        w = 2 * (F + 2)
                        mm = pe.matmul(feat[g % 2][:, q * w:(q + 1) * w], hT[:, 2 * (g % 2) + q, :],
                                       wpair.rearrange("p a b -> p (a b)"), start=True, stop=True)
                    mm.then_inc(feat_done, 1)
                pe.wait_ge(feat_read, GROUPS * (l + 1))
                for b in range(BLOCKS):
                    mm = pe.matmul(acc[1][:, 0:F], ones, xs[:, b, :], start=(b == 0), stop=(b == BLOCKS - 1))
                mm.then_inc(mean_done, 1)
                pe.wait_ge(dmax_ready, l + 1)
                pe.transpose(acc[0][0:1, 0:P], one_col[:, 0:1], identity[:]).then_inc(dmax_turned, 1)
                pe.wait_ge(top_ready, l + 1)
                pe.matmul(acc[0][:, 0:1], ones[0:1, :], one_col[0:1, 3:4], start=True, stop=True
                          ).then_inc(top_spread, 1)
                pe.wait_ge(thr_ready, l + 1)
                pe.transpose(acc[0][0:BLOCKS, 0:P], cols[:, 7, :], identity[:]).then_inc(thr_turned, 1)

                def pack_chunk(k, c):
                    n = l * TILES * CHUNKS + k * CHUNKS + c
                    half, first_in_half = c // HALF_CHUNKS, c % HALF_CHUNKS == 0
                    if first_in_half and not (l == 0 and isinstance(k, int) and k == 0):
                        pe.wait_ge(words_read, 2 * (l * TILES + k) + half - 1)
                    pe.wait_ge(sign_ready, n + 1)
                    if l == 0:
                        pe.wait_ge(mask_ready, n + 1)
                    pe.nop(nofuse=True)
                    for b in range(CHUNK_BLOCKS):
                        at = (c % HALF_CHUNKS) * CHUNK_BLOCKS + b
                        for kind, tiles, slots in ((0, mask, MASK_SLOTS), (1, sign, SIGN_SLOTS)):
                            if kind == 0 and l == 1:
                                continue
                            mm = pe.matmul(pack[half][:, kind, at * WORDS:(at + 1) * WORDS],
                                           tiles[:, c % slots, b * P:(b + 1) * P], powers[:],
                                           start=True, stop=True)
                    mm.then_inc(chunk_packed, 1)

                def product(k, w, packing):
                    n = l * TILES + k
                    pe.wait_ge(mat_ready[w], n + 1)
                    if not (l == 0 and isinstance(k, int) and k == 0):
                        pe.wait_ge(sums_ready[w], n)
                    pe.nop(nofuse=True)
                    for b in range(BLOCKS):
                        mm = pe.matmul(acc[w][:, 0:COLS], work[:, w, b, :],
                                       values[:, w, b, :, :].rearrange("p t c -> p (t c)"),
                                       start=(b == 0), stop=(b == BLOCKS - 1))
                        if b == BLOCKS - 1:
                            mm.then_inc(mat_used[w], 1)
                        if b % MAIN_PER_CHUNK == MAIN_PER_CHUNK - 1 and packing is not None:
                            kk, c0 = packing
                            pack_chunk(kk, c0 + b // MAIN_PER_CHUNK)

                def tile(k, next1=True, next2=True):
                    product(k, 0, (k + 1, HALF_CHUNKS) if next1 else None)
                    product(k, 1, (k + 2, 0) if next2 else None)

                for c in range(CHUNKS):
                    pack_chunk(0, c)
                for c in range(HALF_CHUNKS):
                    pack_chunk(1, c)
                pe.wait_ge(values_ready, l + 1)
                tile(0)
                with pe.Fori(1, TILES - 2) as k:
                    tile(k)
                tile(TILES - 2, next2=False)
                tile(TILES - 1, next1=False, next2=False)

        @block.vector
        def _(dve):
            done = [0]

            def link(ins):
                done[0] += 1
                ins.then_inc(step, 1)
                dve.wait_ge(step, done[0])

            def per_row(col):
                return col.unsqueeze(2).to_broadcast([P, BLOCKS, F])

            for l, (_, _, slope) in enumerate(LAYERS):
                nc.vector.memset(ones, 1.0)
                nc.vector.memset(wpair, 0.0).then_inc(params_free, 1)
                dve.wait_ge(x_loaded, 16 * (l + 1))
                link(nc.vector.tensor_reduce(cols[:, 0, :], xs, AX.X, ALU.add))
                link(nc.vector.tensor_scalar(cols[:, 1, :], cols[:, 0, :], 1.0 / F, None, ALU.mult))
                link(nc.vector.tensor_tensor(xs, xs, per_row(cols[:, 1, :]), ALU.subtract))
                link(nc.vector.tensor_tensor(hs, xs, xs, ALU.mult))
                link(nc.vector.tensor_reduce(cols[:, 2, :], hs, AX.X, ALU.add))
                nc.vector.tensor_scalar(cols[:, 0, :], cols[:, 2, :], 1.0 / F, EPS, ALU.mult, ALU.add
                                        ).then_inc(var_ready, 1)
                dve.wait_ge(std_ready, l + 1)
                link(nc.vector.reciprocal(cols[:, 2, :], cols[:, 1, :]))
                nc.vector.scalar_tensor_tensor(hs, xs, 0.0, per_row(cols[:, 2, :]), ALU.max, ALU.mult
                                               ).then_inc(h_ready, 1)
                if l == 0:
                    dve.wait_ge(consts_in, 32)
                    link(nc.vector.tensor_copy(powers[:], powers_f[:]))
                dve.wait_ge(params_in, 16 * 5 * (l + 1))
                nc.vector.memset(one_col[:, 3:4], 0.0).then_inc(w_ready, 1)
                dve.wait_ge(wt_done, l + 1)
                nc.vector.tensor_copy(wT, acc[0][0:F, 0:P]).then_inc(wt_ready, 1)
                dve.wait_ge(wa_done, l + 1)
                for h in range(2):
                    ins = nc.vector.tensor_copy(wpair[h * F:(h + 1) * F, h, F:F + 2],
                                                acc[1][h * F:(h + 1) * F, 0:2])
                ins.then_inc(wpair_ready, 1)
                for g in range(GROUPS):
                    dve.wait_ge(feat_done, GROUPS * l + g + 1)
                    src = feat[g % 2][:, 0:GROUP * (F + 2)].rearrange("p (b c) -> p b c", b=GROUP)
                    nc.vector.tensor_copy(xs[:, GROUP * g:GROUP * (g + 1), :], src[:, :, 0:F])
                    nc.vector.tensor_copy(sd[:, GROUP * g:GROUP * (g + 1), :], src[:, :, F:F + 2]
                                          ).then_inc(feat_read, 1)
                dve.wait_ge(feat_read, GROUPS * (l + 1))
                s, d = sd[:, :, 0], sd[:, :, 1]
                nc.vector.tensor_reduce(one_col[:, 0:1], d, AX.X, ALU.max).then_inc(dmax_ready, 1)
                dve.wait_ge(mean_done, l + 1)
                nc.vector.tensor_scalar(mean_wh[:], acc[1][:, 0:F], 1.0 / N, None, ALU.mult)
                dve.wait_ge(dmax_turned, l + 1)
                nc.vector.tensor_reduce(one_col[0:1, 3:4], acc[0][0:1, 0:P], AX.X, ALU.max).then_inc(top_ready, 1)
                dve.wait_ge(top_spread, l + 1)
                link(nc.vector.tensor_scalar(one_col[:, 1:2], acc[0][:, 0:1], -1.0, SHIFT, ALU.mult, ALU.add))
                link(nc.vector.tensor_scalar(one_col[:, 2:3], one_col[:, 1:2], slope, None, ALU.mult))
                link(nc.vector.tensor_scalar(cols[:, 6, :], s, one_col[:, 1:2], 1.0 - slope, ALU.subtract, ALU.mult))
                nc.vector.tensor_scalar(cols[:, 4, :], cols[:, 6, :], 0.0, None, ALU.min)
                nc.vector.tensor_scalar(cols[:, 5, :], cols[:, 6, :], -1.0, 0.0, ALU.mult, ALU.min
                                        ).then_inc(exp_args, 1)
                for v, to in ((d, cols[:, 7, :]), (s, s_row[:])):
                    link(nc.vector.tensor_tensor(cols[:, 0, :], v, v, ALU.mult))
                    link(nc.vector.tensor_scalar(cols[:, 0, :], cols[:, 0, :], NEAR_ZERO ** 2, None, ALU.is_ge))
                    link(nc.vector.tensor_tensor(cols[:, 1, :], v, cols[:, 0, :], ALU.mult))
                    if v is d:
                        link(nc.vector.tensor_scalar(cols[:, 1, :].bitcast(U32), cols[:, 1, :].bitcast(U32),
                                                     1, None, ALU.bitwise_or))
                        link(nc.vector.tensor_scalar(cols[:, 0, :], cols[:, 0, :], -TINY, TINY, ALU.mult, ALU.add))
                        nc.vector.tensor_tensor(to, cols[:, 1, :], cols[:, 0, :], ALU.add).then_inc(thr_ready, 1)
                        dve.wait_ge(thr_turned, l + 1)
                        nc.vector.tensor_copy(dT, acc[0][0:BLOCKS, 0:P]).then_inc(dT_ready, 1)
                    else:
                        link(nc.vector.tensor_scalar(to.bitcast(U32), cols[:, 1, :].bitcast(U32),
                                                     1, 1, ALU.logical_shift_right, ALU.logical_shift_left))
                dve.wait_ge(factors_ready, l + 1)
                for w in range(2):
                    f = cols[:, 2 + w, :]
                    rest = cols[:, 6, :]
                    v = values[:, w]
                    link(nc.vector.tensor_tensor(hs, xs, per_row(f), ALU.mult))
                    link(nc.vector.tensor_copy(v[:, :, 0, 0:F], hs))
                    link(nc.vector.tensor_tensor(hs, hs, v[:, :, 0, 0:F], ALU.subtract))
                    link(nc.vector.tensor_copy(v[:, :, 1, 0:F], hs))
                    link(nc.vector.tensor_tensor(v[:, :, 2, 0:F], hs, v[:, :, 1, 0:F], ALU.subtract))
                    link(nc.vector.tensor_copy(v[:, :, 0, F], f))
                    link(nc.vector.tensor_tensor(rest, f, v[:, :, 0, F], ALU.subtract))
                    link(nc.vector.tensor_copy(v[:, :, 1, F], rest))
                    link(nc.vector.tensor_tensor(v[:, :, 2, F], rest, v[:, :, 1, F], ALU.subtract))
                nc.vector.memset(one_col[:, 0:1], 0.0).then_inc(values_ready, 1)

                def masks(k, *chunks):
                    if l == 1:
                        return
                    for c in chunks:
                        n = k * CHUNKS + c
                        loads = CHUNKS // ADJ_SLOTS * k + c // ADJ_SLOTS + 1
                        dve.wait_ge(adj_loaded[c % ADJ_SLOTS], 16 * loads)
                        if not (isinstance(k, int) and n < MASK_SLOTS):
                            dve.wait_ge(chunk_packed, n - (MASK_SLOTS - 1))
                        dve.nop(nofuse=True)
                        nc.vector.tensor_scalar(mask[:, c % MASK_SLOTS, :], adj_in[:, c % ADJ_SLOTS, :], 0.0, None,
                                                ALU.is_gt, saturate=False).then_inc(mask_ready, 1)

                def read_words(k, half):
                    n = l * TILES + k
                    dve.wait_ge(chunk_packed, n * CHUNKS + (half + 1) * HALF_CHUNKS)
                    if l == 0:
                        nc.vector.tensor_copy(packed[:, bass.ds(k * TW + half * HW, HW)], pack[half][:, 0, :])
                    if not (l == 0 and isinstance(k, int) and k == 0):
                        dve.wait_ge(mat_ready[1], n)
                    nc.vector.tensor_scalar(sign_words[:, half * HW:(half + 1) * HW], pack[half][:, 1, :],
                                            float(2 ** BITS - 1), 0.5, ALU.add, ALU.mult).then_inc(words_read, 1)

                def split_words(k):
                    n = l * TILES + k
                    if not (l == 0 and isinstance(k, int) and k == 0):
                        dve.wait_ge(mat_ready[0], n)
                    dve.wait_ge(words_read, 2 * n + 2)
                    here = packed[:, bass.ds(k * TW, TW)]
                    nc.vector.tensor_tensor(steep_words[:], here, sign_words[:], ALU.bitwise_and
                                            ).then_inc(split_step, 1)
                    dve.wait_ge(split_step, 2 * n + 1)
                    nc.vector.tensor_tensor(shallow_words[:], here, steep_words[:], ALU.bitwise_xor
                                            ).then_inc(split_step, 1)

                def unpack(k, w):
                    n = l * TILES + k
                    if not (l == 0 and isinstance(k, int) and k == 0):
                        dve.wait_ge(mat_used[w], n)
                    dve.wait_ge(split_step, 2 * n + 1 + w)
                    words = (steep_words, shallow_words)[w][:].rearrange("p (b g) -> p b g", b=BLOCKS)
                    to = work[:, w].bitcast(U16)
                    for b in range(BITS // 2):
                        if b <= 6:
                            shift, op = 6 - b, ALU.logical_shift_left
                        else:
                            shift, op = b - 6, ALU.logical_shift_right
                        ins = nc.vector.tensor_scalar(to[:, :, b * WORDS:(b + 1) * WORDS], words, shift,
                                                      TWO_TWICE, op, ALU.bitwise_and)
                    ins.then_inc(mat_ready[w], 1)

                def epilogue(k, part):
                    n = l * TILES + k
                    at = [0 if part == 0 else 6]

                    def then(ins):
                        at[0] += 1
                        ins.then_inc(epi, 1)
                        dve.wait_ge(epi, n * EPI_STEPS + at[0])

                    if part == 0:
                        if not (l == 0 and isinstance(k, int) and k == 0):
                            dve.wait_ge(epi, n * EPI_STEPS)
                            dve.wait_ge(out_ready, n)
                        dve.wait_ge(sums_ready[0], n + 1)
                        dve.wait_ge(sums_ready[1], n + 1)
                        ins = nc.vector.tensor_reduce(total[:], sums[:].rearrange("p w (t c) -> p c (w t)", t=3),
                                                      AX.X, ALU.add)
                        ins.then_inc(sums_used, 1)
                        dve.wait_ge(sums_used, n + 1)
                        den, empty, full, inv = total[:, F:F + 1], e_small[:, 0:1], e_small[:, 1:2], e_small[:, 2:3]
                        then(nc.vector.tensor_scalar(empty, den, 0.0, None, ALU.is_equal))
                        then(nc.vector.tensor_tensor(full, den, empty, ALU.add))
                        then(nc.vector.reciprocal(inv, full))
                        then(nc.vector.tensor_scalar(e_mid[:, 0, :], total[:, 0:F], inv, None, ALU.mult))
                        then(nc.vector.scalar_tensor_tensor(e_mid[:, 0, :], mean_wh[:], empty, e_mid[:, 0, :],
                                                            ALU.mult, ALU.add))
                        nc.vector.tensor_scalar(e_mid[:, 1, :], e_mid[:, 0, :], 0.0, None, ALU.min
                                                ).then_inc(neg_ready, 1)
                        nc.vector.tensor_scalar(e_mid[:, 0, :], e_mid[:, 0, :], 0.0, -1.0, ALU.max, ALU.add
                                                ).then_inc(epi, 1)
                    else:
                        dve.wait_ge(epi, n * EPI_STEPS + 6)
                        dve.wait_ge(exp_ready, n + 1)
                        then(nc.vector.tensor_tensor(e_mid[:, 0, :], e_mid[:, 0, :], e_mid[:, 2, :], ALU.add))
                        dve.wait_ge(x_in_loaded, 16 * (n + 1))
                        if not (l == 0 and isinstance(k, int) and k == 0):
                            dve.wait_ge(out_stored, 16 * n)
                        nc.vector.tensor_tensor(x_out[:], e_mid[:, 0, :], x_in[:], ALU.add).then_inc(out_ready, 1)

                def tile(k, first=False, next1=True, next2=True):
                    H = HALF_CHUNKS
                    if next1:
                        masks(k + 1, H, H + 1)
                    unpack(k, 1)
                    if next1:
                        read_words(k + 1, 0)
                        masks(k + 1, H + 2)
                    if not first:
                        epilogue(k - 1, 0)
                    if next1:
                        masks(k + 1, H + 3)
                    if not first:
                        epilogue(k - 1, 1)
                    if next2:
                        masks(k + 2, 0, 1)
                    if next1:
                        read_words(k + 1, 1)
                        split_words(k + 1)
                        unpack(k + 1, 0)
                    if next2:
                        masks(k + 2, 2, 3)

                dve.wait_ge(thr_stored, 16 * (l + 1))
                masks(0, *range(HALF_CHUNKS))
                masks(0, *range(HALF_CHUNKS, CHUNKS))
                read_words(0, 0)
                masks(1, 0, 1)
                read_words(0, 1)
                split_words(0)
                unpack(0, 0)
                masks(1, *range(2, HALF_CHUNKS))
                tile(0, first=True)
                with dve.Fori(1, TILES - 2) as k:
                    tile(k)
                tile(TILES - 2, next2=False)
                tile(TILES - 1, next1=False, next2=False)
                epilogue(TILES - 1, 0)
                epilogue(TILES - 1, 1)


_INS = ["x", "adj", "L0_gnn_W", "L0_gnn_a", "L1_gnn_W", "L1_gnn_a"]


def kernel(**inputs):
    import concourse.bacc as _bacc
    from concourse import mybir as _mybir
    from concourse.bass_utils import run_bass_kernel_spmd as _run

    nc = _bacc.Bacc("TRN2", target_bir_lowering=False, num_devices=1)
    given = {name: np.ascontiguousarray(inputs[name]) for name in _INS}
    rows = np.arange(P)
    given["identity"] = np.eye(P, dtype=np.float32)
    given["powers"] = np.where((rows[:, None] % BITS) // 2 == np.arange(WORDS)[None, :],
                               2.0 ** (8 * (rows[:, None] % 2) + rows[:, None] // BITS), 0.0).astype(np.float32)
    arrays, args = {}, []
    for name, a in given.items():
        arrays[f"in_{name}"] = a
        args.append(nc.dram_tensor(f"in_{name}", a.shape, _mybir.dt.from_np(a.dtype), kind="ExternalInput").ap())
    n, f = given["x"].shape
    args.append(nc.dram_tensor("out_x", (n, f), _mybir.dt.float32, kind="ExternalOutput").ap())
    two_layer_graph_attention(nc, *args)
    r = _run(nc, [arrays], core_ids=[0])
    return r.results[0]["out_x"]
```

```python
from contextlib import ExitStack
from math import exp

import numpy as np

import concourse.bass as bass
from concourse import mybir


P = 128
BITS = 16
WORDS = P // BITS
CHUNK_BLOCKS = 8
CHUNK = CHUNK_BLOCKS * P
ADJ_SLOTS = 8
EARLY_SLOTS = 4
MASK_SLOTS = 4
SIGN_SLOTS = 2
EPS = 1e-5
LO = 2.0 ** 11
TOP = 2.0 ** 14
SHIFT = 32.0
TINY = 2.0 ** -61
NEAR_ZERO = 2.0 ** -60
TWO_TWICE = 0x4040

ALU = mybir.AluOpType
ACT = mybir.ActivationFunctionType
AX = mybir.AxisListType
BF16 = mybir.dt.bfloat16
FP16 = mybir.dt.float16
FP8 = mybir.dt.float8e4
F32 = mybir.dt.float32
I32 = mybir.dt.int32
U16 = mybir.dt.uint16
U32 = mybir.dt.uint32


def two_layer_graph_attention(nc, x, adj, W0, a0, W1, a1, identity_in, powers_in, out):
    N, F = x.shape
    TILES = N // P
    BLOCKS = N // P
    CHUNKS = N // CHUNK
    HALF_CHUNKS = CHUNKS // 2
    HB = BLOCKS // 2
    MAIN_PER_CHUNK = BLOCKS // HALF_CHUNKS
    TW = BLOCKS * WORDS
    HW = TW // 2
    C1 = F + 1
    PARTS = (3, 2)
    COLS = [p * C1 for p in PARTS]
    GROUP = 4
    GROUPS = BLOCKS // GROUP
    LAYERS = ((W0, a0, 0.2), (W1, a1, 0.01))

    x1 = nc.dram_tensor("x_after_layer0", (N, F), F32).ap()
    threshold_dram = [nc.dram_tensor(f"threshold{l}", (BLOCKS, P), F32).ap() for l in range(2)]

    with ExitStack() as ctx:
        def sb(name, shape, dt):
            return ctx.enter_context(nc.sbuf_tensor(name, shape, dt))

        def ps(name, shape, dt=F32):
            return ctx.enter_context(nc.psum_tensor(name, shape, dt))

        def sem(name):
            return ctx.enter_context(nc.semaphore(name))

        packed = sb("packed_adj", [P, TILES * TW], U16)
        steep_values = sb("steep_values", [P, BLOCKS, 3, C1], BF16)
        shallow_values = sb("shallow_values", [P, BLOCKS, 2, C1], FP16)
        values = [steep_values, shallow_values]
        thresholds = sb("thresholds", [P, N], F32)
        work = sb("work", [P, 2, BLOCKS, P], FP8)
        adj_in = sb("adj_in", [P, ADJ_SLOTS, CHUNK], I32)
        mask = sb("mask", [P, MASK_SLOTS, CHUNK], FP8)
        sign = sb("sign", [P, SIGN_SLOTS, CHUNK], BF16)
        sign_words = sb("sign_words", [P, TW], U16)
        steep_words = sb("steep_words", [P, TW], U16)
        shallow_words = sign_words
        identity = sb("identity", [P, P], F32)
        powers_f = sb("powers_f", [P, WORDS], F32)
        powers = sb("powers", [P, WORDS], BF16)
        s_row = sb("s_row", [P, TILES], F32)
        scale_a = sb("scale_a", [P, TILES], F32)
        scale_c = sb("scale_c", [P, TILES], F32)
        mean_wh = sb("mean_wh", [P, F], F32)
        scale_c_lo = sb("scale_c_lo", [P, TILES], F32)
        sums = sb("sums", [P, sum(PARTS), C1], F32)
        total = sb("total", [P, C1], F32)
        e_small = sb("e_small", [P, 4], F32)
        e_mid = sb("e_mid", [P, 3, F], F32)
        x_in = sb("x_in", [P, F], F32)
        x_out = sb("x_out", [P, F], F32)
        xs = work[:].rearrange("p a b c -> p (a b c)").bitcast(F32).rearrange("p (b f) -> p b f", b=BLOCKS)
        ts = adj_in[:, 0:EARLY_SLOTS, :].rearrange("p a b -> p (a b)").bitcast(F32).rearrange("p (b f) -> p b f", b=BLOCKS)
        hs = adj_in[:, EARLY_SLOTS:, :].rearrange("p a b -> p (a b)").bitcast(F32).rearrange("p (b f) -> p b f", b=BLOCKS)
        hT = sign[:].rearrange("p a b -> p (a b)").bitcast(F32).rearrange("p (s c) -> p s c", c=P)
        small = mask[:].rearrange("p a b -> p (a b)").bitcast(F32)
        cols = small[:, 0:8 * BLOCKS].rearrange("p (a b) -> p a b", a=8)
        sd = small[:, 8 * BLOCKS:10 * BLOCKS].rearrange("p (b t) -> p b t", t=2)
        wT = small[0:F, 10 * BLOCKS:10 * BLOCKS + P]
        dT = small[0:BLOCKS, 10 * BLOCKS + P:10 * BLOCKS + 2 * P]
        spare = sums[:].rearrange("p a b -> p (a b)")
        ones = spare[:, 0:P]
        wpair = spare[:, P:P + 2 * (F + 2)].rearrange("p (a b) -> p a b", a=2)
        w_twice = spare[:, P + 2 * (F + 2):P + 2 * (F + 2) + F]
        a_cols = sb("a_cols", [F, 2], F32)
        one_col = sb("one_col", [P, 8], F32)
        pair = sb("pair", [2, 2], F32)

        acc = [ps("acc_steep", [P, 512]), ps("acc_shallow", [P, 512])]
        pack = [ps(f"pack{h}", [P, 2, HW]) for h in range(2)]
        turn = [ps(f"turn{h}", [P, 512]) for h in range(2)]
        feat = [ps(f"feat{h}", [P, 512]) for h in range(2)]

        consts_in = sem("consts_in")
        params_in = sem("params_in")
        adj_loaded = [sem(f"adj_loaded{i}") for i in range(ADJ_SLOTS)]
        x_loaded = [sem(f"x_loaded{h}") for h in range(2)]
        row_squares = sem("row_squares")
        norm_done = sem("norm_done")
        norm_ready = sem("norm_ready")
        centred = sem("centred")
        squared = sem("squared")
        thr_rows_ready = sem("thr_rows_ready")
        scaled = sem("scaled")
        part_cut = sem("part_cut")
        thr_stored = sem("thr_stored")
        thr_loaded = sem("thr_loaded")
        step = sem("dve_step")
        params_free = sem("params_free")
        wt_done = sem("wt_done")
        wt_ready = sem("wt_ready")
        wa_done = sem("wa_done")
        wpair_ready = sem("wpair_ready")
        var_ready = sem("var_ready")
        std_ready = sem("std_ready")
        h_ready = sem("h_ready")
        turned = sem("turned")
        hT_ready = sem("hT_ready")
        feat_done = sem("feat_done")
        feat_read = sem("feat_read")
        mean_done = sem("mean_done")
        dmax_ready = sem("dmax_ready")
        dmax_turned = sem("dmax_turned")
        top_ready = sem("top_ready")
        top_spread = sem("top_spread")
        exp_args = sem("exp_args")
        factors_ready = sem("factors_ready")
        thr_ready = sem("thr_ready")
        thr_turned = sem("thr_turned")
        dT_ready = sem("dT_ready")
        values_ready = sem("values_ready")
        mask_ready = sem("mask_ready")
        sign_ready = sem("sign_ready")
        chunk_packed = sem("chunk_packed")
        words_read = sem("words_read")
        split_step = sem("split_step")
        mat_ready = [sem("steep_ready"), sem("shallow_ready")]
        mat_used = [sem("steep_used"), sem("shallow_used")]
        sums_ready = [sem("steep_sums"), sem("shallow_sums")]
        sums_used = sem("sums_used")
        epi = sem("epilogue_step")
        neg_ready = sem("neg_ready")
        exp_ready = sem("exp_ready")
        out_ready = sem("out_ready")
        x_in_loaded = sem("x_in_loaded")
        out_stored = sem("out_stored")

        EPI_STEPS = 7
        block = ctx.enter_context(nc.Block())

        @block.sync
        def _(sp):
            sp.dma_start(identity[:], identity_in).then_inc(consts_in, 16)
            sp.dma_start(powers_f[:], powers_in).then_inc(consts_in, 16)

            def load_adj(k):
                for c in range(CHUNKS):
                    sp.wait_ge(mask_ready, CHUNKS * k + (c - ADJ_SLOTS + 1))
                    sp.dma_start(adj_in[:, c % ADJ_SLOTS, :],
                                 adj[bass.ds(k * P, P), c * CHUNK:(c + 1) * CHUNK]
                                 ).then_inc(adj_loaded[c % ADJ_SLOTS], 16)

            for l, (W, a, _) in enumerate(LAYERS):
                sp.wait_ge(params_free, l + 1)
                for h in range(2):
                    sp.dma_start(w_twice[h * F:(h + 1) * F, :], W).then_inc(params_in, 16)
                    sp.dma_start(wpair[h * F:(h + 1) * F, h, 0:F], W).then_inc(params_in, 16)
                sp.dma_start(a_cols[:], a.rearrange("(t o) u -> o (t u)", t=2),
                             allow_slow_non_contiguous=True).then_inc(params_in, 16)
                if l == 1:
                    sp.wait_ge(out_stored, 16 * TILES)
                    sp.wait_ge(mat_used[0], TILES)
                    sp.wait_ge(mat_used[1], TILES)
                src = x if l == 0 else x1
                for h in range(2):
                    sp.dma_start(xs[:, HB * h:HB * (h + 1), :],
                                 src.rearrange("(b p) f -> p b f", p=P)[:, HB * h:HB * (h + 1), :]
                                 ).then_inc(x_loaded[h], 16)
                sp.wait_ge(dT_ready, l + 1)
                sp.dma_start(threshold_dram[l], dT).then_inc(thr_stored, 16)
                sp.wait_ge(thr_stored, 16 * (l + 1))
                if l == 1:
                    sp.wait_ge(sign_ready, CHUNKS * TILES)
                sp.dma_start(thresholds[:], threshold_dram[l].rearrange("b p -> (b p)").partition_broadcast(P)
                             ).then_inc(thr_loaded, 16)
                if l == 0:
                    sp.wait_ge(part_cut, 3)
                    for c in range(EARLY_SLOTS):
                        sp.dma_start(adj_in[:, c, :], adj[0:P, c * CHUNK:(c + 1) * CHUNK]
                                     ).then_inc(adj_loaded[c], 16)
                    sp.wait_ge(values_ready, 1)
                    for c in range(EARLY_SLOTS, CHUNKS):
                        sp.dma_start(adj_in[:, c % ADJ_SLOTS, :], adj[0:P, c * CHUNK:(c + 1) * CHUNK]
                                     ).then_inc(adj_loaded[c % ADJ_SLOTS], 16)
                    with sp.Fori(1, TILES) as k:
                        load_adj(k)

        @block.gpsimd
        def _(pool):
            for l in range(2):
                src = x if l == 0 else x1
                dst = x1 if l == 0 else out

                def rows(k, first=False):
                    if not first:
                        pool.wait_ge(out_ready, l * TILES + k)
                    pool.nop(nofuse=True)
                    pool.dma_start(x_in[:], src[bass.ds(k * P, P), :]).then_inc(x_in_loaded, 16)
                    pool.wait_ge(out_ready, l * TILES + k + 1)
                    pool.nop(nofuse=True)
                    pool.dma_start(dst[bass.ds(k * P, P), :], x_out[:]).then_inc(out_stored, 16)

                if l == 1:
                    pool.wait_ge(out_stored, 16 * TILES)
                rows(0, first=(l == 0))
                with pool.Fori(1, TILES) as k:
                    rows(k)
            pool.wait_ge(out_stored, 16 * 2 * TILES)

        @block.scalar
        def _(act):
            for l, (_, _, slope) in enumerate(LAYERS):
                act.wait_ge(norm_done, l + 1)
                nc.scalar.activation(one_col[:, 4:5], acc[1][:, 2:3], ACT.Sqrt, scale=F / 2.0).then_inc(norm_ready, 1)
                for h in range(2):
                    half = slice(HB * h, HB * (h + 1))
                    act.wait_ge(centred, 2 * l + h + 1)
                    nc.scalar.activation(hs[:, half, :], xs[:, half, :], ACT.Square).then_inc(squared, 1)
                act.wait_ge(var_ready, l + 1)
                nc.scalar.activation(cols[:, 1, :], cols[:, 0, :], ACT.Sqrt).then_inc(std_ready, 1)
                for g in range(GROUPS):
                    act.wait_ge(turned, GROUPS * l + g + 1)
                    if g >= 2:
                        act.wait_ge(feat_done, GROUPS * l + g - 1)
                    nc.scalar.copy(hT[:, 2 * (g % 2):2 * (g % 2) + 2, :].rearrange("p a b -> p (a b)")
                                   , turn[g % 2][:, 0:2 * P]).then_inc(hT_ready, 1)
                act.wait_ge(exp_args, l + 1)
                d = sd[:, :, 1]
                nc.scalar.activation(cols[:, 2, :], d, ACT.Exp, bias=one_col[:, 1:2], scale=1.0)
                nc.scalar.activation(cols[:, 3, :], d, ACT.Exp, bias=one_col[:, 2:3], scale=slope)
                nc.scalar.activation(scale_a[:], cols[:, 4, :], ACT.Exp)
                nc.scalar.activation(cols[:, 5, :], cols[:, 5, :], ACT.Exp).then_inc(factors_ready, 1)
                for n, (to, src, by) in enumerate((
                        (shallow_values[:, :, 0, 0:F], ts, 1.0), (steep_values[:, :, 0, 0:F], hs, 1.0),
                        (shallow_values[:, :, 1, 0:F], ts, LO), (steep_values[:, :, 1, 0:F], hs, 1.0))):
                    act.wait_ge(scaled, 4 * l + n + 1)
                    nc.scalar.activation(to, src, ACT.Copy, scale=by).then_inc(part_cut, 1)
                act.wait_ge(thr_rows_ready, l + 1)
                act.wait_ge(thr_loaded, 16 * (l + 1))

                def signs(k, c):
                    n = l * TILES * CHUNKS + k * CHUNKS + c
                    if not (l == 0 and isinstance(k, int) and n < SIGN_SLOTS):
                        act.wait_ge(chunk_packed, n - (SIGN_SLOTS - 1))
                    act.nop(nofuse=True)
                    nc.scalar.activation(sign[:, c % SIGN_SLOTS, :], thresholds[:, c * CHUNK:(c + 1) * CHUNK],
                                         ACT.Sign, bias=s_row[:, bass.ds(k, 1)]).then_inc(sign_ready, 1)

                def scaled_sums(k, w):
                    n = l * TILES + k
                    act.wait_ge(mat_used[w], n + 1)
                    if not (l == 0 and isinstance(k, int) and k == 0):
                        act.wait_ge(sums_used, n)
                    act.nop(nofuse=True)
                    if w == 0:
                        ins = nc.scalar.activation(sums[:, 0:3, :].rearrange("p t c -> p (t c)"), acc[0][:, 0:COLS[0]],
                                                   ACT.Copy, scale=scale_a[:, bass.ds(k, 1)])
                    else:
                        nc.scalar.activation(sums[:, 3, :], acc[1][:, 0:C1], ACT.Copy, scale=scale_c[:, bass.ds(k, 1)])
                        ins = nc.scalar.activation(sums[:, 4, :], acc[1][:, C1:2 * C1], ACT.Copy,
                                                   scale=scale_c_lo[:, bass.ds(k, 1)])
                    ins.then_inc(sums_ready[w], 1)

                def negative_exp(k):
                    act.wait_ge(neg_ready, l * TILES + k + 1)
                    nc.scalar.activation(e_mid[:, 2, :], e_mid[:, 1, :], ACT.Exp).then_inc(exp_ready, 1)

                def tile(k, first=False, next1=True, next2=True):
                    if not first:
                        scaled_sums(k - 1, 1)
                    for c in range(HALF_CHUNKS, CHUNKS):
                        if next1:
                            signs(k + 1, c)
                        if c == CHUNKS - 2 and not first:
                            negative_exp(k - 1)
                    if next2:
                        signs(k + 2, 0)
                        signs(k + 2, 1)
                    scaled_sums(k, 0)
                    if next2:
                        for c in range(2, HALF_CHUNKS):
                            signs(k + 2, c)

                for c in range(CHUNKS):
                    signs(0, c)
                for c in range(HALF_CHUNKS):
                    signs(1, c)
                tile(0, first=True)
                with act.Fori(1, TILES - 2) as k:
                    tile(k)
                tile(TILES - 2, next2=False)
                tile(TILES - 1, next1=False, next2=False)
                scaled_sums(TILES - 1, 1)
                negative_exp(TILES - 1)

        @block.tensor
        def _(pe):
            pe.wait_ge(consts_in, 32)
            for l in range(2):
                pe.wait_ge(params_in, 16 * 5 * (l + 1))
                pe.transpose(acc[0][0:F, 0:P], w_twice, identity[:]).then_inc(wt_done, 1)
                pe.wait_ge(wt_ready, l + 1)
                pe.matmul(acc[1][:, 0:2], wT, a_cols[:], start=True, stop=True).then_inc(wa_done, 1)
                pe.wait_ge(row_squares, l + 1)
                pe.matmul(acc[1][:, 2:3], ones, one_col[:, 4:5], start=True, stop=True).then_inc(norm_done, 1)
                pe.wait_ge(wpair_ready, l + 1)
                def turn_group(g):
                    pe.wait_ge(h_ready, 2 * l + (g >= GROUPS // 2) + 1)
                    if g >= 2:
                        pe.wait_ge(hT_ready, GROUPS * l + g - 1)
                    for q in range(2):
                        b = GROUP * g + 2 * q
                        mm = pe.transpose(turn[g % 2][:, q * P:(q + 1) * P],
                                          hs[:, b:b + 2, :].rearrange("p b f -> p (b f)"), identity[:])
                    mm.then_inc(turned, 1)

                turn_group(0)
                for g in range(GROUPS):
                    if g + 1 < GROUPS:
                        turn_group(g + 1)
                    pe.wait_ge(hT_ready, GROUPS * l + g + 1)
                    if g >= 2:
                        pe.wait_ge(feat_read, GROUPS * l + g - 1)
                    for q in range(2):
                        w = 2 * (F + 2)
                        mm = pe.matmul(feat[g % 2][:, q * w:(q + 1) * w], hT[:, 2 * (g % 2) + q, :],
                                       wpair.rearrange("p a b -> p (a b)"), start=True, stop=True)
                    mm.then_inc(feat_done, 1)
                pe.wait_ge(dmax_ready, l + 1)
                pe.transpose(acc[0][0:1, 0:P], one_col[:, 0:1], identity[:]).then_inc(dmax_turned, 1)
                pe.wait_ge(top_ready, l + 1)
                pe.matmul(acc[0][:, 0:1], ones[0:1, :], pair[0:1, 0:1], start=True, stop=True
                          ).then_inc(top_spread, 1)
                pe.wait_ge(thr_ready, l + 1)
                pe.transpose(acc[0][0:BLOCKS, 0:P], cols[:, 7, :], identity[:]).then_inc(thr_turned, 1)

                pe.wait_ge(feat_read, GROUPS * (l + 1))
                for b in range(BLOCKS):
                    mm = pe.matmul(acc[1][:, 0:F], ones, xs[:, b, :], start=(b == 0), stop=(b == BLOCKS - 1))
                mm.then_inc(mean_done, 1)

                def pack_chunk(k, c):
                    n = l * TILES * CHUNKS + k * CHUNKS + c
                    half, first_in_half = c // HALF_CHUNKS, c % HALF_CHUNKS == 0
                    if first_in_half and not (l == 0 and isinstance(k, int) and k == 0):
                        pe.wait_ge(words_read, 2 * (l * TILES + k) + half - 1)
                    pe.wait_ge(sign_ready, n + 1)
                    if l == 0:
                        pe.wait_ge(mask_ready, n + 1)
                    pe.nop(nofuse=True)
                    for b in range(CHUNK_BLOCKS):
                        at = (c % HALF_CHUNKS) * CHUNK_BLOCKS + b
                        for kind, tiles, slots in ((0, mask, MASK_SLOTS), (1, sign, SIGN_SLOTS)):
                            if kind == 0 and l == 1:
                                continue
                            mm = pe.matmul(pack[half][:, kind, at * WORDS:(at + 1) * WORDS],
                                           tiles[:, c % slots, b * P:(b + 1) * P], powers[:],
                                           start=True, stop=True)
                    mm.then_inc(chunk_packed, 1)

                def product(k, w, packing):
                    n = l * TILES + k
                    pe.wait_ge(mat_ready[w], n + 1)
                    if not (l == 0 and isinstance(k, int) and k == 0):
                        pe.wait_ge(sums_ready[w], n)
                    pe.nop(nofuse=True)
                    for b in range(BLOCKS):
                        mm = pe.matmul(acc[w][:, 0:COLS[w]], work[:, w, b, :],
                                       values[w][:, b, :, :].rearrange("p t c -> p (t c)"),
                                       start=(b == 0), stop=(b == BLOCKS - 1))
                        if b == BLOCKS - 1:
                            mm.then_inc(mat_used[w], 1)
                        if b % MAIN_PER_CHUNK == MAIN_PER_CHUNK - 1 and packing is not None:
                            kk, c0 = packing
                            pack_chunk(kk, c0 + b // MAIN_PER_CHUNK)

                def tile(k, next1=True, next2=True):
                    product(k, 0, (k + 1, HALF_CHUNKS) if next1 else None)
                    product(k, 1, (k + 2, 0) if next2 else None)

                for c in range(CHUNKS):
                    pack_chunk(0, c)
                for c in range(HALF_CHUNKS):
                    pack_chunk(1, c)
                pe.wait_ge(values_ready, l + 1)
                tile(0)
                with pe.Fori(1, TILES - 2) as k:
                    tile(k)
                tile(TILES - 2, next2=False)
                tile(TILES - 1, next1=False, next2=False)

        @block.vector
        def _(dve):
            done = [0]

            def link(ins):
                done[0] += 1
                ins.then_inc(step, 1)
                dve.wait_ge(step, done[0])

            def per_row(col):
                return col.unsqueeze(2).to_broadcast([P, BLOCKS, F])

            for l, (_, _, slope) in enumerate(LAYERS):
                nc.vector.memset(ones, 1.0)
                nc.vector.memset(wpair, 0.0).then_inc(params_free, 1)
                if l == 0:
                    dve.wait_ge(consts_in, 32)
                    link(nc.vector.tensor_copy(powers[:], powers_f[:]))
                dve.wait_ge(params_in, 16 * 5 * (l + 1))
                link(nc.vector.tensor_tensor(total[:, 0:F], w_twice, w_twice, ALU.mult))
                nc.vector.tensor_reduce(one_col[:, 4:5], total[:, 0:F], AX.X, ALU.add).then_inc(row_squares, 1)
                dve.wait_ge(wt_done, l + 1)
                nc.vector.tensor_copy(wT, acc[0][0:F, 0:P]).then_inc(wt_ready, 1)
                dve.wait_ge(wa_done, l + 1)
                dve.wait_ge(norm_ready, l + 1)
                for h in range(2):
                    ins = nc.vector.tensor_copy(wpair[h * F:(h + 1) * F, h, F:F + 2],
                                                acc[1][h * F:(h + 1) * F, 0:2])
                ins.then_inc(wpair_ready, 1)
                halves = [slice(HB * h, HB * (h + 1)) for h in range(2)]

                def half_row(i, h):
                    return cols[:, i, halves[h]].unsqueeze(2).to_broadcast([P, HB, F])

                for h in range(2):
                    dve.wait_ge(x_loaded[h], 16 * (l + 1))
                    link(nc.vector.tensor_reduce(cols[:, 0, halves[h]], xs[:, halves[h], :], AX.X, ALU.add))
                    link(nc.vector.tensor_scalar(cols[:, 1, halves[h]], cols[:, 0, halves[h]], 1.0 / F, None, ALU.mult))
                    nc.vector.tensor_tensor(xs[:, halves[h], :], xs[:, halves[h], :], half_row(1, h), ALU.subtract
                                            ).then_inc(centred, 1)
                for h in range(2):
                    dve.wait_ge(squared, 2 * l + h + 1)
                    link(nc.vector.tensor_reduce(cols[:, 2, halves[h]], hs[:, halves[h], :], AX.X, ALU.add))
                nc.vector.tensor_scalar(cols[:, 0, :], cols[:, 2, :], 1.0 / F, EPS, ALU.mult, ALU.add
                                        ).then_inc(var_ready, 1)
                dve.wait_ge(std_ready, l + 1)
                link(nc.vector.reciprocal(cols[:, 2, :], cols[:, 1, :]))
                for h in range(2):
                    nc.vector.scalar_tensor_tensor(hs[:, halves[h], :], xs[:, halves[h], :], 0.0, half_row(2, h),
                                                   ALU.max, ALU.mult).then_inc(h_ready, 1)
                for g in range(GROUPS):
                    dve.wait_ge(feat_done, GROUPS * l + g + 1)
                    src = feat[g % 2][:, 0:GROUP * (F + 2)].rearrange("p (b c) -> p b c", b=GROUP)
                    nc.vector.tensor_copy(xs[:, GROUP * g:GROUP * (g + 1), :], src[:, :, 0:F])
                    nc.vector.tensor_copy(sd[:, GROUP * g:GROUP * (g + 1), :], src[:, :, F:F + 2]
                                          ).then_inc(feat_read, 1)
                dve.wait_ge(feat_read, GROUPS * (l + 1))
                s, d = sd[:, :, 0], sd[:, :, 1]
                nc.vector.tensor_reduce(one_col[:, 0:1], d, AX.X, ALU.max).then_inc(dmax_ready, 1)
                dve.wait_ge(norm_ready, l + 1)
                link(nc.vector.tensor_scalar(one_col[:, 3:4], one_col[:, 4:5], 1.0, None, ALU.max))
                link(nc.vector.reciprocal(one_col[:, 6:7], one_col[:, 3:4]))
                link(nc.vector.tensor_scalar(one_col[:, 7:8], one_col[:, 6:7], TOP, None, ALU.mult))
                dve.wait_ge(dmax_turned, l + 1)
                nc.vector.tensor_reduce(pair[0:1, 0:1], acc[0][0:1, 0:P], AX.X, ALU.max).then_inc(top_ready, 1)
                dve.wait_ge(top_spread, l + 1)
                link(nc.vector.tensor_scalar(one_col[:, 1:2], acc[0][:, 0:1], -1.0, SHIFT, ALU.mult, ALU.add))
                link(nc.vector.tensor_scalar(one_col[:, 2:3], acc[0][:, 0:1], -slope, None, ALU.mult))
                link(nc.vector.tensor_scalar(cols[:, 6, :], s, one_col[:, 1:2], 1.0 - slope, ALU.subtract, ALU.mult))
                nc.vector.tensor_scalar(cols[:, 4, :], cols[:, 6, :], 0.0, None, ALU.min)
                nc.vector.tensor_scalar(cols[:, 5, :], cols[:, 6, :], -1.0, 0.0, ALU.mult, ALU.min
                                        ).then_inc(exp_args, 1)
                for v, to in ((d, cols[:, 7, :]), (s, s_row[:])):
                    link(nc.vector.tensor_tensor(cols[:, 0, :], v, v, ALU.mult))
                    link(nc.vector.tensor_scalar(cols[:, 0, :], cols[:, 0, :], NEAR_ZERO ** 2, None, ALU.is_ge))
                    link(nc.vector.tensor_tensor(cols[:, 1, :], v, cols[:, 0, :], ALU.mult))
                    if v is d:
                        link(nc.vector.tensor_scalar(cols[:, 1, :].bitcast(U32), cols[:, 1, :].bitcast(U32),
                                                     1, None, ALU.bitwise_or))
                        link(nc.vector.tensor_scalar(cols[:, 0, :], cols[:, 0, :], -TINY, TINY, ALU.mult, ALU.add))
                        nc.vector.tensor_tensor(to, cols[:, 1, :], cols[:, 0, :], ALU.add).then_inc(thr_ready, 1)
                        dve.wait_ge(thr_turned, l + 1)
                        nc.vector.tensor_copy(dT, acc[0][0:BLOCKS, 0:P]).then_inc(dT_ready, 1)
                    else:
                        nc.vector.tensor_scalar(to.bitcast(U32), cols[:, 1, :].bitcast(U32), 1, 1,
                                                ALU.logical_shift_right, ALU.logical_shift_left
                                                ).then_inc(thr_rows_ready, 1)
                dve.wait_ge(factors_ready, l + 1)
                steep_f, shallow_f, rest = cols[:, 2, :], cols[:, 3, :], cols[:, 6, :]
                link(nc.vector.tensor_scalar(shallow_f, shallow_f, one_col[:, 7:8], None, ALU.mult))
                nc.vector.tensor_tensor(ts, xs, per_row(shallow_f), ALU.mult).then_inc(scaled, 1)
                nc.vector.tensor_tensor(hs, xs, per_row(steep_f), ALU.mult).then_inc(scaled, 1)
                link(nc.vector.tensor_scalar(scale_c[:], cols[:, 5, :], one_col[:, 3:4], exp(slope * SHIFT) / TOP,
                                             ALU.mult, ALU.mult))
                nc.vector.tensor_scalar(scale_c_lo[:], scale_c[:], 1.0 / LO, None, ALU.mult)
                v = shallow_values[:, :, :, F]
                link(nc.vector.tensor_copy(v[:, :, 0], shallow_f))
                link(nc.vector.tensor_tensor(rest, shallow_f, v[:, :, 0], ALU.subtract))
                nc.vector.tensor_scalar(v[:, :, 1], rest, LO, None, ALU.mult)
                dve.wait_ge(part_cut, 4 * l + 1)
                nc.vector.tensor_tensor(ts, ts, shallow_values[:, :, 0, 0:F], ALU.subtract).then_inc(scaled, 1)
                dve.wait_ge(part_cut, 4 * l + 2)
                nc.vector.tensor_tensor(hs, hs, steep_values[:, :, 0, 0:F], ALU.subtract).then_inc(scaled, 1)
                v, rest = steep_values[:, :, :, F], cols[:, 7, :]
                link(nc.vector.tensor_copy(v[:, :, 0], steep_f))
                link(nc.vector.tensor_tensor(rest, steep_f, v[:, :, 0], ALU.subtract))
                link(nc.vector.tensor_copy(v[:, :, 1], rest))
                link(nc.vector.tensor_tensor(v[:, :, 2], rest, v[:, :, 1], ALU.subtract))
                dve.wait_ge(mean_done, l + 1)
                link(nc.vector.tensor_scalar(mean_wh[:], acc[1][:, 0:F], 1.0 / N, None, ALU.mult))
                dve.wait_ge(part_cut, 4 * l + 4)
                nc.vector.tensor_tensor(steep_values[:, :, 2, 0:F], hs, steep_values[:, :, 1, 0:F], ALU.subtract
                                        ).then_inc(values_ready, 1)

                def masks(k, *chunks):
                    if l == 1:
                        return
                    for c in chunks:
                        n = k * CHUNKS + c
                        loads = CHUNKS // ADJ_SLOTS * k + c // ADJ_SLOTS + 1
                        dve.wait_ge(adj_loaded[c % ADJ_SLOTS], 16 * loads)
                        if not (isinstance(k, int) and n < MASK_SLOTS):
                            dve.wait_ge(chunk_packed, n - (MASK_SLOTS - 1))
                        dve.nop(nofuse=True)
                        nc.vector.tensor_scalar(mask[:, c % MASK_SLOTS, :], adj_in[:, c % ADJ_SLOTS, :], 0.0, None,
                                                ALU.is_gt, saturate=False).then_inc(mask_ready, 1)

                def read_words(k, half):
                    n = l * TILES + k
                    dve.wait_ge(chunk_packed, n * CHUNKS + (half + 1) * HALF_CHUNKS)
                    if l == 0:
                        nc.vector.tensor_copy(packed[:, bass.ds(k * TW + half * HW, HW)], pack[half][:, 0, :])
                    if not (l == 0 and isinstance(k, int) and k == 0):
                        dve.wait_ge(mat_ready[1], n)
                    nc.vector.tensor_scalar(sign_words[:, half * HW:(half + 1) * HW], pack[half][:, 1, :],
                                            float(2 ** BITS - 1), 0.5, ALU.add, ALU.mult).then_inc(words_read, 1)

                def split_words(k):
                    n = l * TILES + k
                    if not (l == 0 and isinstance(k, int) and k == 0):
                        dve.wait_ge(mat_ready[0], n)
                    dve.wait_ge(words_read, 2 * n + 2)
                    here = packed[:, bass.ds(k * TW, TW)]
                    nc.vector.tensor_tensor(steep_words[:], here, sign_words[:], ALU.bitwise_and
                                            ).then_inc(split_step, 1)
                    dve.wait_ge(split_step, 2 * n + 1)
                    nc.vector.tensor_tensor(shallow_words[:], here, steep_words[:], ALU.bitwise_xor
                                            ).then_inc(split_step, 1)

                def unpack(k, w):
                    n = l * TILES + k
                    if not (l == 0 and isinstance(k, int) and k == 0):
                        dve.wait_ge(mat_used[w], n)
                    dve.wait_ge(split_step, 2 * n + 1 + w)
                    words = (steep_words, shallow_words)[w][:].rearrange("p (b g) -> p b g", b=BLOCKS)
                    to = work[:, w].bitcast(U16)
                    for b in range(BITS // 2):
                        if b <= 6:
                            shift, op = 6 - b, ALU.logical_shift_left
                        else:
                            shift, op = b - 6, ALU.logical_shift_right
                        ins = nc.vector.tensor_scalar(to[:, :, b * WORDS:(b + 1) * WORDS], words, shift,
                                                      TWO_TWICE, op, ALU.bitwise_and)
                    ins.then_inc(mat_ready[w], 1)

                def epilogue(k, part):
                    n = l * TILES + k
                    at = [0 if part == 0 else 6]

                    def then(ins):
                        at[0] += 1
                        ins.then_inc(epi, 1)
                        dve.wait_ge(epi, n * EPI_STEPS + at[0])

                    if part == 0:
                        if not (l == 0 and isinstance(k, int) and k == 0):
                            dve.wait_ge(epi, n * EPI_STEPS)
                            dve.wait_ge(out_ready, n)
                        dve.wait_ge(sums_ready[0], n + 1)
                        dve.wait_ge(sums_ready[1], n + 1)
                        ins = nc.vector.tensor_reduce(total[:], sums[:].rearrange("p t c -> p c t"),
                                                      AX.X, ALU.add)
                        ins.then_inc(sums_used, 1)
                        dve.wait_ge(sums_used, n + 1)
                        den, empty, full, inv = total[:, F:F + 1], e_small[:, 0:1], e_small[:, 1:2], e_small[:, 2:3]
                        then(nc.vector.tensor_scalar(empty, den, 0.0, None, ALU.is_equal))
                        then(nc.vector.tensor_tensor(full, den, empty, ALU.add))
                        then(nc.vector.reciprocal(inv, full))
                        then(nc.vector.tensor_scalar(e_mid[:, 0, :], total[:, 0:F], inv, None, ALU.mult))
                        then(nc.vector.scalar_tensor_tensor(e_mid[:, 0, :], mean_wh[:], empty, e_mid[:, 0, :],
                                                            ALU.mult, ALU.add))
                        nc.vector.tensor_scalar(e_mid[:, 1, :], e_mid[:, 0, :], 0.0, None, ALU.min
                                                ).then_inc(neg_ready, 1)
                        nc.vector.tensor_scalar(e_mid[:, 0, :], e_mid[:, 0, :], 0.0, -1.0, ALU.max, ALU.add
                                                ).then_inc(epi, 1)
                    else:
                        dve.wait_ge(epi, n * EPI_STEPS + 6)
                        dve.wait_ge(exp_ready, n + 1)
                        then(nc.vector.tensor_tensor(e_mid[:, 0, :], e_mid[:, 0, :], e_mid[:, 2, :], ALU.add))
                        dve.wait_ge(x_in_loaded, 16 * (n + 1))
                        if not (l == 0 and isinstance(k, int) and k == 0):
                            dve.wait_ge(out_stored, 16 * n)
                        nc.vector.tensor_tensor(x_out[:], e_mid[:, 0, :], x_in[:], ALU.add).then_inc(out_ready, 1)

                def tile(k, first=False, next1=True, next2=True):
                    H = HALF_CHUNKS
                    if next1:
                        masks(k + 1, H, H + 1)
                    unpack(k, 1)
                    if next1:
                        read_words(k + 1, 0)
                        masks(k + 1, H + 2)
                    if not first:
                        epilogue(k - 1, 0)
                    if next1:
                        masks(k + 1, H + 3)
                    if not first:
                        epilogue(k - 1, 1)
                    if next2:
                        masks(k + 2, 0, 1)
                    if next1:
                        read_words(k + 1, 1)
                        split_words(k + 1)
                        unpack(k + 1, 0)
                    if next2:
                        masks(k + 2, 2, 3)

                dve.wait_ge(thr_stored, 16 * (l + 1))
                masks(0, *range(HALF_CHUNKS))
                masks(0, *range(HALF_CHUNKS, CHUNKS))
                read_words(0, 0)
                masks(1, 0, 1)
                read_words(0, 1)
                split_words(0)
                unpack(0, 0)
                masks(1, *range(2, HALF_CHUNKS))
                tile(0, first=True)
                with dve.Fori(1, TILES - 2) as k:
                    tile(k)
                tile(TILES - 2, next2=False)
                tile(TILES - 1, next1=False, next2=False)
                epilogue(TILES - 1, 0)
                epilogue(TILES - 1, 1)


_INS = ["x", "adj", "L0_gnn_W", "L0_gnn_a", "L1_gnn_W", "L1_gnn_a"]


def kernel(**inputs):
    import concourse.bacc as _bacc
    from concourse import mybir as _mybir
    from concourse.bass_utils import run_bass_kernel_spmd as _run

    nc = _bacc.Bacc("TRN2", target_bir_lowering=False, num_devices=1)
    given = {name: np.ascontiguousarray(inputs[name]) for name in _INS}
    rows = np.arange(P)
    given["identity"] = np.eye(P, dtype=np.float32)
    given["powers"] = np.where((rows[:, None] % BITS) // 2 == np.arange(WORDS)[None, :],
                               2.0 ** (8 * (rows[:, None] % 2) + rows[:, None] // BITS), 0.0).astype(np.float32)
    arrays, args = {}, []
    for name, a in given.items():
        arrays[f"in_{name}"] = a
        args.append(nc.dram_tensor(f"in_{name}", a.shape, _mybir.dt.from_np(a.dtype), kind="ExternalInput").ap())
    n, f = given["x"].shape
    args.append(nc.dram_tensor("out_x", (n, f), _mybir.dt.float32, kind="ExternalOutput").ap())
    two_layer_graph_attention(nc, *args)
    r = _run(nc, [arrays], core_ids=[0])
    return r.results[0]["out_x"]
```

```python
from contextlib import ExitStack
from math import exp

import numpy as np

import concourse.bass as bass
from concourse import mybir


P = 128
BITS = 16
WORDS = P // BITS
CHUNK_BLOCKS = 8
CHUNK = CHUNK_BLOCKS * P
ADJ_SLOTS = 8
MASK_SLOTS = 4
SIGN_SLOTS = 4
EARLY_SIGNS = 2
EPS = 1e-5
LO = 2.0 ** 11
TOP = 2.0 ** 14
SHIFT = 32.0
NARROW = 12.0
TINY = 2.0 ** -61
NEAR_ZERO = 2.0 ** -60
TWO_TWICE = 0x4040

ALU = mybir.AluOpType
ACT = mybir.ActivationFunctionType
AX = mybir.AxisListType
BF16 = mybir.dt.bfloat16
FP16 = mybir.dt.float16
FP8 = mybir.dt.float8e4
F32 = mybir.dt.float32
I32 = mybir.dt.int32
U16 = mybir.dt.uint16
U32 = mybir.dt.uint32


def two_layer_graph_attention(nc, x, adj, W0, a0, W1, a1, identity_in, powers_in, out):
    N, F = x.shape
    TILES = N // P
    BLOCKS = N // P
    CHUNKS = N // CHUNK
    HALF_CHUNKS = CHUNKS // 2
    TW = BLOCKS * WORDS
    HW = TW // 2
    C1 = F + 1
    WIDE_PARTS, PARTS = 3, 2
    NORM_PARTS = [(BLOCKS * a // 8, BLOCKS * b // 8) for a, b in ((0, 2), (2, 4), (4, 7), (7, 8))]
    LAST = len(NORM_PARTS) - 1
    GROUP = 4
    GROUPS = BLOCKS // GROUP
    LAYERS = ((W0, a0, 0.2), (W1, a1, 0.01))

    x1 = nc.dram_tensor("x_after_layer0", (N, F), F32).ap()
    threshold_dram = [nc.dram_tensor(f"threshold{l}", (BLOCKS, P), F32).ap() for l in range(2)]

    with ExitStack() as ctx:
        def sb(name, shape, dt):
            return ctx.enter_context(nc.sbuf_tensor(name, shape, dt))

        def ps(name, shape, dt=F32):
            return ctx.enter_context(nc.psum_tensor(name, shape, dt))

        def sem(name):
            return ctx.enter_context(nc.semaphore(name))

        packed = sb("packed_adj", [P, TILES * TW], U16)
        steep_wide = sb("steep_values", [P, BLOCKS, WIDE_PARTS, C1], BF16)[:]
        steep_narrow = steep_wide.rearrange("p b t c -> p (b t c)").bitcast(FP16)[:, 0:BLOCKS * PARTS * C1].rearrange(
            "p (b t c) -> p b t c", b=BLOCKS, t=PARTS)
        shallow_values = sb("shallow_values", [P, BLOCKS, PARTS, C1], FP16)[:]
        thresholds = sb("thresholds", [P, N], F32)
        work = sb("work", [P, 2, BLOCKS, P], FP8)
        adj_in = sb("adj_in", [P, ADJ_SLOTS, CHUNK], I32)
        mask = sb("mask", [P, MASK_SLOTS, CHUNK], FP8)
        sign = sb("sign", [P, SIGN_SLOTS, CHUNK], BF16)
        sign_words = sb("sign_words", [P, TW], U16)
        steep_words = sb("steep_words", [P, TW], U16)
        shallow_words = sb("shallow_words", [P, TW], U16)
        identity = sb("identity", [P, P], F32)
        powers_f = sb("powers_f", [P, WORDS], F32)
        powers = sb("powers", [P, WORDS], BF16)
        s_row = sb("s_row", [P, TILES], F32)
        scale_a = sb("scale_a", [P, TILES], F32)
        scale_c = sb("scale_c", [P, TILES], F32)
        mean_wh = sb("mean_wh", [P, F], F32)
        scale_c_lo = sb("scale_c_lo", [P, TILES], F32)
        sums = sb("sums", [P, PARTS + WIDE_PARTS, C1], F32)
        scale_a_lo = sb("scale_a_lo", [P, TILES], F32)
        total = sb("total", [P, C1], F32)
        e_small = sb("e_small", [P, 4], F32)
        e_mid = sb("e_mid", [P, 4, F], F32)
        x_in = sb("x_in", [P, F], F32)
        x_out = sb("x_out", [P, F], F32)
        xs = work[:].rearrange("p a b c -> p (a b c)").bitcast(F32).rearrange("p (b f) -> p b f", b=BLOCKS)
        scratch = []
        for space in (packed[:].bitcast(F32), adj_in[:].rearrange("p a b -> p (a b)").bitcast(F32)):
            end = space.shape[1]
            scratch.append([space[:, end - (2 - i) * BLOCKS * F:end - (1 - i) * BLOCKS * F].rearrange(
                "p (b f) -> p b f", b=BLOCKS) for i in range(2)])
        hT = sign[:, 0:2, :].rearrange("p a b -> p (a b)").bitcast(F32).rearrange("p (s c) -> p s c", c=P)
        small = []
        for space in (packed[:, 0:TILES * TW // 2].bitcast(F32), mask[:].rearrange("p a b -> p (a b)").bitcast(F32)):
            space = space[:, space.shape[1] - 10 * BLOCKS - 2 * P:]
            small.append((space[:, 0:8 * BLOCKS].rearrange("p (a b) -> p a b", a=8),
                          space[:, 8 * BLOCKS:10 * BLOCKS].rearrange("p (b t) -> p b t", t=2),
                          space[0:F, 10 * BLOCKS:10 * BLOCKS + P],
                          space[0:BLOCKS, 10 * BLOCKS + P:10 * BLOCKS + 2 * P]))
        ones = sb("ones", [P, P], F32)[:]
        wpair = sb("wpair", [P, 2, F + 2], F32)[:]
        w_twice = sb("w_twice", [P, F], F32)[:]
        a_cols = sb("a_cols", [F, 2], F32)
        one_col = sb("one_col", [P, 13], F32)
        top = sb("top", [2, 1], F32)
        flag = sb("narrow_flag", [1, 2], I32)
        h_sums = sb("h_sums", [P, GROUPS], F32)
        h_mean = sb("h_mean", [P, 1], F32)
        mean_lhs = sb("mean_lhs", [P, P], F32)

        acc = [ps("acc_steep", [P, 512]), ps("acc_shallow", [P, 512])]
        pack = [ps(f"pack{h}", [P, 2, HW]) for h in range(2)]
        turn = [ps(f"turn{h}", [P, 512]) for h in range(2)]
        feat = [ps(f"feat{h}", [P, 512]) for h in range(2)]

        consts_in = sem("consts_in")
        params_in = sem("params_in")
        adj_loaded = [sem(f"adj_loaded{i}") for i in range(ADJ_SLOTS)]
        x_loaded = [sem(f"x_loaded{h}") for h in range(len(NORM_PARTS))]
        row_squares = sem("row_squares")
        norm_done = sem("norm_done")
        h_mean_ready = sem("h_mean_ready")
        elu_step = sem("elu_step")
        norm_ready = sem("norm_ready")
        centred = sem("centred")
        squared = sem("squared")
        thr_rows_ready = sem("thr_rows_ready")
        scaled = sem("scaled")
        steep_cut = sem("steep_cut")
        shallow_cut = sem("shallow_cut")
        thr_stored = sem("thr_stored")
        thr_loaded = [sem(f"thr_loaded{h}") for h in range(2)]
        step = sem("dve_step")
        params_zeroed = sem("params_zeroed")
        wt_done = sem("wt_done")
        wt_ready = sem("wt_ready")
        wa_done = sem("wa_done")
        wpair_ready = sem("wpair_ready")
        var_ready = sem("var_ready")
        std_ready = sem("std_ready")
        h_ready = sem("h_ready")
        turned = sem("turned")
        hT_ready = sem("hT_ready")
        feat_done = sem("feat_done")
        feat_read = sem("feat_read")
        mean_done = sem("mean_done")
        dmax_ready = sem("dmax_ready")
        dmax_turned = sem("dmax_turned")
        top_ready = sem("top_ready")
        top_spread = sem("top_spread")
        flag_ready = sem("flag_ready")
        exp_args = sem("exp_args")
        factors_ready = sem("factors_ready")
        thr_ready = sem("thr_ready")
        thr_turned = sem("thr_turned")
        dT_ready = sem("dT_ready")
        values_ready = sem("values_ready")
        mask_ready = sem("mask_ready")
        sign_ready = sem("sign_ready")
        chunk_packed = sem("chunk_packed")
        words_read = [sem(f"words_read{h}") for h in range(2)]
        split_step = sem("split_step")
        mat_ready = [sem("steep_ready"), sem("shallow_ready")]
        mat_used = [sem("steep_used"), sem("shallow_used")]
        sums_ready = [sem("steep_sums"), sem("shallow_sums")]
        sums_used = sem("sums_used")
        epi = sem("epilogue_step")
        neg_ready = sem("neg_ready")
        exp_ready = sem("exp_ready")
        out_ready = sem("out_ready")
        x_in_loaded = sem("x_in_loaded")
        out_stored = sem("out_stored")

        EPI_STEPS = 5
        block = ctx.enter_context(nc.Block())

        @block.sync
        def _(sp):
            sp.dma_start(identity[:], identity_in).then_inc(consts_in, 16)
            sp.dma_start(powers_f[:], powers_in).then_inc(consts_in, 16)

            def load_adj(k):
                for c in range(CHUNKS):
                    sp.wait_ge(mask_ready, CHUNKS * k + (c - ADJ_SLOTS + 1))
                    sp.dma_start(adj_in[:, c % ADJ_SLOTS, :],
                                 adj[bass.ds(k * P, P), c * CHUNK:(c + 1) * CHUNK]
                                 ).then_inc(adj_loaded[c % ADJ_SLOTS], 16)

            for l, (W, a, _) in enumerate(LAYERS):
                ts, hs = scratch[l]
                cols, sd, wT, dT = small[l]
                src = (x if l == 0 else x1).rearrange("(b p) f -> p b f", p=P)
                def load_params():
                    for q in range(2):
                        sp.dma_start(w_twice[q * F:(q + 1) * F, :], W).then_inc(params_in, 16)
                        sp.dma_start(wpair[q * F:(q + 1) * F, q, 0:F], W).then_inc(params_in, 16)
                    sp.dma_start(a_cols[:], a.rearrange("(t o) u -> o (t u)", t=2),
                                 allow_slow_non_contiguous=True).then_inc(params_in, 16)

                if l == 1:
                    sp.wait_ge(mean_done, 1)
                    load_params()
                    sp.wait_ge(mask_ready, CHUNKS * TILES - HALF_CHUNKS)
                for h, (b0, b1) in enumerate(NORM_PARTS):
                    if h == LAST and l == 0:
                        sp.wait_ge(params_zeroed, 1)
                        load_params()
                    if l == 1:
                        sp.wait_ge(out_stored, 16 * b1)
                    sp.dma_start(ts[:, b0:b1, :], src[:, b0:b1, :]).then_inc(x_loaded[h], 16)
                if l == 0:
                    for c in range(CHUNKS):
                        sp.dma_start(adj_in[:, c, :], adj[0:P, c * CHUNK:(c + 1) * CHUNK]).then_inc(adj_loaded[c], 16)
                sp.wait_ge(dT_ready, l + 1)
                sp.dma_start(threshold_dram[l], dT).then_inc(thr_stored, 16)
                sp.wait_ge(thr_stored, 16 * (l + 1))
                if l == 1:
                    sp.wait_ge(sign_ready, CHUNKS * TILES)
                row = threshold_dram[l].rearrange("b p -> (b p)")
                for h in range(2):
                    here = slice(h * N // 2, (h + 1) * N // 2)
                    sp.dma_start(thresholds[:, here], row[here].partition_broadcast(P)).then_inc(thr_loaded[h], 16)
                if l == 0:
                    with sp.Fori(1, TILES) as k:
                        load_adj(k)

        @block.gpsimd
        def _(pool):
            for l in range(2):
                src = x if l == 0 else x1
                dst = x1 if l == 0 else out

                def rows(k, first=False):
                    if not first:
                        pool.wait_ge(out_ready, l * TILES + k)
                    pool.nop(nofuse=True)
                    pool.dma_start(x_in[:], src[bass.ds(k * P, P), :]).then_inc(x_in_loaded, 16)
                    n = l * TILES + k
                    pool.wait_ge(epi, EPI_STEPS * (n + 1))
                    pool.nop(nofuse=True)
                    nc.gpsimd.tensor_scalar(e_mid[:, 1, :], e_mid[:, 0, :], 0.0, None, ALU.min).then_inc(neg_ready, 1)
                    nc.gpsimd.tensor_scalar(e_mid[:, 3, :], e_mid[:, 0, :], 0.0, -1.0, ALU.max, ALU.add
                                            ).then_inc(elu_step, 1)
                    pool.wait_ge(elu_step, 2 * n + 1)
                    pool.wait_ge(x_in_loaded, 16 * (n + 1))
                    pool.nop(nofuse=True)
                    nc.gpsimd.tensor_tensor(e_mid[:, 3, :], e_mid[:, 3, :], x_in[:], ALU.add).then_inc(elu_step, 1)
                    pool.wait_ge(elu_step, 2 * n + 2)
                    pool.wait_ge(exp_ready, n + 1)
                    if not (l == 0 and isinstance(k, int) and k == 0):
                        pool.wait_ge(out_stored, 16 * n)
                    pool.nop(nofuse=True)
                    nc.gpsimd.tensor_tensor(x_out[:], e_mid[:, 3, :], e_mid[:, 2, :], ALU.add).then_inc(out_ready, 1)
                    pool.wait_ge(out_ready, n + 1)
                    pool.nop(nofuse=True)
                    pool.dma_start(dst[bass.ds(k * P, P), :], x_out[:]).then_inc(out_stored, 16)

                if l == 1:
                    pool.wait_ge(out_stored, 16 * TILES)
                rows(0, first=(l == 0))
                with pool.Fori(1, TILES) as k:
                    rows(k)
            pool.wait_ge(out_stored, 16 * 2 * TILES)

        @block.scalar
        def _(act):
            def square(l, h):
                ts, hs = scratch[l]
                b0, b1 = NORM_PARTS[h]
                act.wait_ge(centred, len(NORM_PARTS) * l + h + 1)
                nc.scalar.activation(hs[:, b0:b1, :], ts[:, b0:b1, :], ACT.Square).then_inc(squared, 1)

            for l, (_, _, slope) in enumerate(LAYERS):
                ts, hs = scratch[l]
                cols, sd, wT, dT = small[l]
                if l == 0:
                    square(0, 0)
                square(l, 1)
                square(l, 2)
                act.wait_ge(norm_done, l + 1)
                nc.scalar.activation(one_col[:, 4:5], feat[0][:, 0:1], ACT.Sqrt, scale=F / 2.0).then_inc(norm_ready, 1)

                def root(h):
                    b0, b1 = NORM_PARTS[h]
                    act.wait_ge(var_ready, len(NORM_PARTS) * l + h + 1)
                    nc.scalar.activation(cols[:, 1, b0:b1], cols[:, 0, b0:b1], ACT.Sqrt).then_inc(std_ready, 1)

                for h in range(LAST):
                    root(h)
                for g in range(GROUPS):
                    if g == 2:
                        square(l, LAST)
                        root(LAST)
                    act.wait_ge(turned, GROUPS * l + g + 1)
                    if g >= 2:
                        act.wait_ge(feat_done, GROUPS * l + g - 1)
                    nc.scalar.activation(hT[:, 2 * (g % 2):2 * (g % 2) + 2, :].rearrange("p a b -> p (a b)"),
                                         turn[g % 2][:, 0:2 * P], ACT.Copy, accum_out=h_sums[:, g:g + 1]
                                         ).then_inc(hT_ready, 1)
                act.wait_ge(exp_args, l + 1)
                d = sd[:, :, 1]
                nc.scalar.activation(cols[:, 2, :], d, ACT.Exp, bias=one_col[:, 1:2], scale=1.0)
                nc.scalar.activation(cols[:, 3, :], d, ACT.Exp, bias=one_col[:, 2:3], scale=slope)
                nc.scalar.activation(scale_a[:], cols[:, 4, :], ACT.Exp)
                nc.scalar.activation(cols[:, 5, :], cols[:, 5, :], ACT.Exp).then_inc(factors_ready, 1)
                def signs(k, c):
                    n = l * TILES * CHUNKS + k * CHUNKS + c
                    if not (l == 0 and isinstance(k, int) and n < SIGN_SLOTS):
                        act.wait_ge(chunk_packed, n - (SIGN_SLOTS - 1))
                    act.nop(nofuse=True)
                    nc.scalar.activation(sign[:, c % SIGN_SLOTS, :], thresholds[:, c * CHUNK:(c + 1) * CHUNK],
                                         ACT.Sign, bias=s_row[:, bass.ds(k, 1)]).then_inc(sign_ready, 1)

                def cut_values(narrow):
                    steep = steep_narrow if narrow else steep_wide
                    for n, (to, src, by, cut) in enumerate((
                            (steep[:, :, 0, 0:F], hs, 1.0, steep_cut), (shallow_values[:, :, 0, 0:F], ts, 1.0, shallow_cut),
                            (steep[:, :, 1, 0:F], hs, LO if narrow else 1.0, steep_cut))):
                        act.wait_ge(scaled, 4 * l + n + 1)
                        nc.scalar.activation(to, src, ACT.Copy, scale=by).then_inc(cut, 1)
                        if n == 1:
                            act.wait_ge(thr_rows_ready, l + 1)
                            act.wait_ge(thr_loaded[0], 16 * (l + 1))
                            for c in range(EARLY_SIGNS):
                                signs(0, c)
                    act.wait_ge(thr_loaded[1], 16 * (l + 1))

                act.wait_ge(flag_ready, l + 1)
                is_narrow = act.value_load(flag[0:1, l:l + 1])
                with act.If(is_narrow == 1):
                    cut_values(True)
                with act.Else():
                    cut_values(False)

                def scaled_sums(k, w, narrow):
                    if l == 1 and w == 1:
                        return
                    n = l * TILES + k
                    act.wait_ge(mat_used[w], n + 1)
                    if not (l == 0 and isinstance(k, int) and k == 0):
                        act.wait_ge(sums_used, n)
                    act.nop(nofuse=True)
                    if w == 0 and not narrow:
                        ins = nc.scalar.activation(sums[:, PARTS:, :].rearrange("p t c -> p (t c)"),
                                                   acc[0][:, 0:WIDE_PARTS * C1], ACT.Copy,
                                                   scale=scale_a[:, bass.ds(k, 1)])
                    else:
                        at, high, low = ((PARTS, scale_a, scale_a_lo), (0, scale_c, scale_c_lo))[w]
                        nc.scalar.activation(sums[:, at, :], acc[w][:, 0:C1], ACT.Copy, scale=high[:, bass.ds(k, 1)])
                        ins = nc.scalar.activation(sums[:, at + 1, :], acc[w][:, C1:2 * C1], ACT.Copy,
                                                   scale=low[:, bass.ds(k, 1)])
                    ins.then_inc(sums_ready[w], 1)

                def read_words(k):
                    if l == 1:
                        return
                    act.wait_ge(chunk_packed, k * CHUNKS + HALF_CHUNKS)
                    if not (isinstance(k, int) and k == 0):
                        act.wait_ge(split_step, 2 * k)
                    act.nop(nofuse=True)
                    nc.scalar.copy(packed[:, bass.ds(k * TW, HW)], pack[0][:, 0, :])
                    nc.scalar.activation(sign_words[:, 0:HW], pack[0][:, 1, :], ACT.Copy,
                                         bias=float(2 ** BITS - 1) / 2, scale=0.5).then_inc(words_read[0], 1)

                def negative_exp(k):
                    act.wait_ge(neg_ready, l * TILES + k + 1)
                    nc.scalar.activation(e_mid[:, 2, :], e_mid[:, 1, :], ACT.Exp).then_inc(exp_ready, 1)

                def tile(k, narrow, first=False, next1=True, next2=True):
                    for c in range(HALF_CHUNKS, CHUNKS):
                        if next1:
                            signs(k + 1, c)
                        if c == HALF_CHUNKS and not first:
                            scaled_sums(k - 1, 1, narrow)
                        if c == HALF_CHUNKS and next1:
                            read_words(k + 1)
                    if next2:
                        signs(k + 2, 0)
                        signs(k + 2, 1)
                    scaled_sums(k, 0, narrow)
                    if not first:
                        negative_exp(k - 1)
                    if next2:
                        for c in range(2, HALF_CHUNKS):
                            signs(k + 2, c)

                def tiles(narrow):
                    tile(0, narrow, first=True)
                    with act.Fori(1, TILES - 2) as k:
                        tile(k, narrow)
                    tile(TILES - 2, narrow, next2=False)
                    tile(TILES - 1, narrow, next1=False, next2=False)

                for c in range(EARLY_SIGNS, CHUNKS):
                    signs(0, c)
                    if c == HALF_CHUNKS + 1:
                        read_words(0)
                for c in range(HALF_CHUNKS):
                    signs(1, c)
                with act.If(is_narrow == 1):
                    tiles(True)
                with act.Else():
                    tiles(False)
                if l == 0:
                    square(1, 0)
                scaled_sums(TILES - 1, 1, True)
                negative_exp(TILES - 1)

        @block.tensor
        def _(pe):
            pe.wait_ge(consts_in, 32)
            for l in range(2):
                _, hs = scratch[l]
                cols, _, wT, _ = small[l]
                pe.wait_ge(params_in, 16 * 5 * (l + 1))
                if l == 1:
                    for w in range(2):
                        pe.wait_ge(sums_ready[w], TILES)
                pe.transpose(acc[0][0:F, 0:P], w_twice, identity[:]).then_inc(wt_done, 1)
                pe.wait_ge(wt_ready, l + 1)
                pe.matmul(acc[1][:, 0:2], wT, a_cols[:], start=True, stop=True).then_inc(wa_done, 1)
                pe.wait_ge(row_squares, l + 1)
                pe.matmul(feat[0][:, 0:1], ones, one_col[:, 4:5], start=True, stop=True).then_inc(norm_done, 1)
                pe.wait_ge(wpair_ready, l + 1)
                pe.wait_ge(norm_ready, l + 1)
                def turn_group(g):
                    part = [GROUP * g < b1 for _, b1 in NORM_PARTS].index(True)
                    pe.wait_ge(h_ready, len(NORM_PARTS) * l + part + 1)
                    if g >= 2:
                        pe.wait_ge(hT_ready, GROUPS * l + g - 1)
                    for q in range(2):
                        b = GROUP * g + 2 * q
                        mm = pe.transpose(turn[g % 2][:, q * P:(q + 1) * P],
                                          hs[:, b:b + 2, :].rearrange("p b f -> p (b f)"), identity[:])
                    mm.then_inc(turned, 1)

                turn_group(0)
                for g in range(GROUPS):
                    if g + 1 < GROUPS:
                        turn_group(g + 1)
                    pe.wait_ge(hT_ready, GROUPS * l + g + 1)
                    if g >= 2:
                        pe.wait_ge(feat_read, GROUPS * l + g - 1)
                    for q in range(2):
                        w = 2 * (F + 2)
                        mm = pe.matmul(feat[g % 2][:, q * w:(q + 1) * w], hT[:, 2 * (g % 2) + q, :],
                                       wpair.rearrange("p a b -> p (a b)"), start=True, stop=True)
                    mm.then_inc(feat_done, 1)
                pe.wait_ge(dmax_ready, l + 1)
                pe.transpose(acc[0][0:2, 0:P], one_col[:, 8:10], identity[:]).then_inc(dmax_turned, 1)
                pe.wait_ge(top_ready, l + 1)
                pe.matmul(acc[0][:, 0:1], ones[0:1, :], top[0:1, :], start=True, stop=True)
                pe.matmul(acc[0][:, 1:2], ones[0:2, :], top[:], start=True, stop=True).then_inc(top_spread, 1)
                pe.wait_ge(thr_ready, l + 1)
                pe.transpose(acc[0][0:BLOCKS, 0:P], cols[:, 7, :], identity[:]).then_inc(thr_turned, 1)

                pe.wait_ge(h_mean_ready, l + 1)
                pe.matmul(acc[1][:, 0:F], mean_lhs[:], w_twice, start=True, stop=True).then_inc(mean_done, 1)

                def pack_chunk(k, c):
                    n = l * TILES * CHUNKS + k * CHUNKS + c
                    half, first_in_half = c // HALF_CHUNKS, c % HALF_CHUNKS == 0
                    if first_in_half and not (l == 0 and isinstance(k, int) and k == 0):
                        pe.wait_ge(words_read[half], l * TILES + k)
                    pe.wait_ge(sign_ready, n + 1)
                    if l == 0:
                        pe.wait_ge(mask_ready, n + 1)
                    pe.nop(nofuse=True)
                    for b in range(CHUNK_BLOCKS):
                        at = (c % HALF_CHUNKS) * CHUNK_BLOCKS + b
                        for kind, tiles, slots in ((0, mask, MASK_SLOTS), (1, sign, SIGN_SLOTS)):
                            if kind == 0 and l == 1:
                                continue
                            mm = pe.matmul(pack[half][:, kind, at * WORDS:(at + 1) * WORDS],
                                           tiles[:, c % slots, b * P:(b + 1) * P], powers[:],
                                           start=True, stop=True)
                    mm.then_inc(chunk_packed, 1)

                def product(k, w, narrow, packing):
                    n = l * TILES + k
                    pe.wait_ge(mat_ready[w], n + 1)
                    if not (l == 0 and isinstance(k, int) and k == 0):
                        pe.wait_ge(sums_ready[w], n)
                    pe.nop(nofuse=True)
                    values = shallow_values if w == 1 else steep_narrow if narrow else steep_wide
                    for b in range(BLOCKS):
                        mm = pe.matmul(acc[w][:, 0:values.shape[2] * C1], work[:, w, b, :],
                                       values[:, b, :, :].rearrange("p t c -> p (t c)"),
                                       start=(b == 0), stop=(b == BLOCKS - 1))
                        if b == BLOCKS - 1:
                            mm.then_inc(mat_used[w], 1)
                        share = BLOCKS // len(packing) if packing else 0
                        if packing and b % share == share - 1:
                            pack_chunk(*packing[b // share])

                def chunks(k, c0, c1):
                    return [(k, c) for c in range(c0, c1)]

                H = HALF_CHUNKS

                def tile(k, narrow, next1=True, next2=True):
                    product(k, 0, narrow, chunks(k + 1, H, CHUNKS) if next1 else [])
                    product(k, 1, narrow, chunks(k + 2, 0, H) if next2 else [])

                def tiles(narrow):
                    product(0, 0, narrow, chunks(1, 0, CHUNKS))
                    product(0, 1, narrow, chunks(2, 0, H))
                    with pe.Fori(1, TILES - 2) as k:
                        tile(k, narrow)
                    tile(TILES - 2, narrow, next2=False)
                    tile(TILES - 1, narrow, next1=False, next2=False)

                for c in range(CHUNKS):
                    pack_chunk(0, c)
                pe.wait_ge(values_ready, l + 1)
                pe.wait_ge(shallow_cut, 2 * (l + 1))
                pe.wait_ge(flag_ready, l + 1)
                is_narrow = pe.value_load(flag[0:1, l:l + 1])
                with pe.If(is_narrow == 1):
                    tiles(True)
                with pe.Else():
                    tiles(False)

        @block.vector
        def _(dve):
            done = [0]

            def link(ins, by=1):
                done[0] += by
                ins.then_inc(step, by)
                dve.wait_ge(step, done[0])

            def per_row(col):
                return col.unsqueeze(2).to_broadcast([P, BLOCKS, F])

            def part_row(cols, i, b0, b1):
                return cols[:, i, b0:b1].unsqueeze(2).to_broadcast([P, b1 - b0, F])

            def centre(l, h):
                ts, hs = scratch[l]
                cols = small[l][0]
                b0, b1 = NORM_PARTS[h]
                dve.wait_ge(x_loaded[h], 16 * (l + 1))
                link(nc.vector.tensor_reduce(cols[:, 0, b0:b1], ts[:, b0:b1, :], AX.X, ALU.add))
                link(nc.vector.tensor_scalar(cols[:, 1, b0:b1], cols[:, 0, b0:b1], 1.0 / F, None, ALU.mult))
                nc.vector.tensor_tensor(ts[:, b0:b1, :], ts[:, b0:b1, :], part_row(cols, 1, b0, b1), ALU.subtract
                                        ).then_inc(centred, 1)

            def variance(l, h):
                ts, hs = scratch[l]
                cols = small[l][0]
                b0, b1 = NORM_PARTS[h]
                dve.wait_ge(squared, len(NORM_PARTS) * l + h + 1)
                link(nc.vector.tensor_reduce(cols[:, 2, b0:b1], hs[:, b0:b1, :], AX.X, ALU.add))
                nc.vector.tensor_scalar(cols[:, 0, b0:b1], cols[:, 2, b0:b1], 1.0 / F, EPS, ALU.mult, ALU.add
                                        ).then_inc(var_ready, 1)

            def normalise(l, h):
                ts, hs = scratch[l]
                cols = small[l][0]
                b0, b1 = NORM_PARTS[h]
                dve.wait_ge(std_ready, len(NORM_PARTS) * l + h + 1)
                link(nc.vector.reciprocal(cols[:, 3, b0:b1], cols[:, 1, b0:b1]))
                nc.vector.scalar_tensor_tensor(hs[:, b0:b1, :], ts[:, b0:b1, :], 0.0, part_row(cols, 3, b0, b1),
                                               ALU.max, ALU.mult).then_inc(h_ready, 1)

            for l, (_, _, slope) in enumerate(LAYERS):
                ts, hs = scratch[l]
                cols, sd, wT, dT = small[l]
                if l == 0:
                    nc.vector.memset(ones, 1.0)
                    nc.vector.memset(wpair, 0.0).then_inc(params_zeroed, 1)
                if l == 0:
                    centre(0, 0)
                    centre(0, 1)
                centre(l, 2)
                if l == 0:
                    dve.wait_ge(consts_in, 32)
                    link(nc.vector.tensor_copy(powers[:], powers_f[:]))
                dve.wait_ge(params_in, 16 * 5 * (l + 1))
                link(nc.vector.tensor_tensor(total[:, 0:F], w_twice, w_twice, ALU.mult))
                nc.vector.tensor_reduce(one_col[:, 4:5], total[:, 0:F], AX.X, ALU.add).then_inc(row_squares, 1)
                dve.wait_ge(wt_done, l + 1)
                nc.vector.tensor_copy(wT, acc[0][0:F, 0:P]).then_inc(wt_ready, 1)
                dve.wait_ge(wa_done, l + 1)
                for h in range(2):
                    ins = nc.vector.tensor_copy(wpair[h * F:(h + 1) * F, h, F:F + 2],
                                                acc[1][h * F:(h + 1) * F, 0:2])
                ins.then_inc(wpair_ready, 1)
                variance(l, 0)
                variance(l, 1)
                normalise(l, 0)
                variance(l, 2)
                normalise(l, 1)
                centre(l, 3)
                normalise(l, 2)
                variance(l, 3)
                for g in range(GROUPS):
                    if g == 2:
                        normalise(l, LAST)
                    dve.wait_ge(feat_done, GROUPS * l + g + 1)
                    src = feat[g % 2][:, 0:GROUP * (F + 2)].rearrange("p (b c) -> p b c", b=GROUP)
                    nc.vector.tensor_copy(xs[:, GROUP * g:GROUP * (g + 1), :], src[:, :, 0:F])
                    nc.vector.tensor_copy(sd[:, GROUP * g:GROUP * (g + 1), :], src[:, :, F:F + 2]
                                          ).then_inc(feat_read, 1)
                dve.wait_ge(feat_read, GROUPS * (l + 1))
                s, d = sd[:, :, 0], sd[:, :, 1]
                link(nc.vector.tensor_reduce(one_col[:, 12:13], d, AX.X, ALU.min))
                nc.vector.tensor_reduce(one_col[:, 8:9], d, AX.X, ALU.max)
                nc.vector.tensor_scalar(one_col[:, 9:10], one_col[:, 12:13], -1.0, None, ALU.mult
                                        ).then_inc(dmax_ready, 1)
                dve.wait_ge(norm_ready, l + 1)
                link(nc.vector.tensor_scalar(one_col[:, 3:4], one_col[:, 4:5], 1.0, None, ALU.max))
                link(nc.vector.reciprocal(one_col[:, 6:7], one_col[:, 3:4]))
                link(nc.vector.tensor_scalar(one_col[:, 7:8], one_col[:, 6:7], TOP, None, ALU.mult))
                dve.wait_ge(dmax_turned, l + 1)
                nc.vector.tensor_reduce(top[:], acc[0][0:2, 0:P], AX.X, ALU.max).then_inc(top_ready, 1)
                dve.wait_ge(top_spread, l + 1)
                link(nc.vector.tensor_scalar(one_col[:, 1:2], acc[0][:, 0:1], -1.0, SHIFT, ALU.mult, ALU.add))
                link(nc.vector.tensor_scalar(one_col[:, 2:3], acc[0][:, 0:1], -slope, None, ALU.mult))
                link(nc.vector.tensor_scalar(one_col[:, 0:1], acc[0][:, 1:2], NARROW, None, ALU.is_le))
                nc.vector.tensor_copy(flag[0:1, l:l + 1], one_col[0:1, 0:1]).then_inc(flag_ready, 1)
                link(nc.vector.tensor_scalar(cols[:, 6, :], s, one_col[:, 1:2], 1.0 - slope, ALU.subtract, ALU.mult))
                nc.vector.tensor_scalar(cols[:, 4, :], cols[:, 6, :], 0.0, None, ALU.min)
                nc.vector.tensor_scalar(cols[:, 5, :], cols[:, 6, :], -1.0, 0.0, ALU.mult, ALU.min
                                        ).then_inc(exp_args, 1)
                for v, to in ((d, cols[:, 7, :]), (s, s_row[:])):
                    link(nc.vector.tensor_tensor(cols[:, 0, :], v, v, ALU.mult))
                    link(nc.vector.tensor_scalar(cols[:, 0, :], cols[:, 0, :], NEAR_ZERO ** 2, None, ALU.is_ge))
                    link(nc.vector.tensor_tensor(cols[:, 1, :], v, cols[:, 0, :], ALU.mult))
                    if v is d:
                        link(nc.vector.tensor_scalar(cols[:, 1, :].bitcast(U32), cols[:, 1, :].bitcast(U32),
                                                     1, None, ALU.bitwise_or))
                        link(nc.vector.tensor_scalar(cols[:, 0, :], cols[:, 0, :], -TINY, TINY, ALU.mult, ALU.add))
                        nc.vector.tensor_tensor(to, cols[:, 1, :], cols[:, 0, :], ALU.add).then_inc(thr_ready, 1)
                        dve.wait_ge(thr_turned, l + 1)
                        nc.vector.tensor_copy(dT, acc[0][0:BLOCKS, 0:P]).then_inc(dT_ready, 1)
                    else:
                        nc.vector.tensor_scalar(to.bitcast(U32), cols[:, 1, :].bitcast(U32), 1, 1,
                                                ALU.logical_shift_right, ALU.logical_shift_left
                                                ).then_inc(thr_rows_ready, 1)
                link(nc.vector.tensor_scalar(one_col[:, 5:6], one_col[:, 0:1], -1.0, 1.0, ALU.mult, ALU.add))
                for to, of, by in ((10, 7, exp(-SHIFT)), (11, 3, exp(SHIFT) / TOP)):
                    link(nc.vector.tensor_scalar(one_col[:, to:to + 1], one_col[:, of:of + 1], one_col[:, 0:1], by,
                                                 ALU.mult, ALU.mult))
                link(nc.vector.tensor_scalar(one_col[:, 10:12], one_col[:, 10:12], one_col[:, 5:6], None, ALU.add))
                dve.wait_ge(factors_ready, l + 1)
                steep_f, shallow_f, rest = cols[:, 2, :], cols[:, 3, :], cols[:, 6, :]
                link(nc.vector.tensor_scalar(steep_f, steep_f, one_col[:, 10:11], None, ALU.mult))
                nc.vector.tensor_tensor(hs, xs, per_row(steep_f), ALU.mult).then_inc(scaled, 1)
                link(nc.vector.tensor_scalar(shallow_f, shallow_f, one_col[:, 7:8], None, ALU.mult))
                nc.vector.tensor_tensor(ts, xs, per_row(shallow_f), ALU.mult).then_inc(scaled, 1)
                link(nc.vector.tensor_reduce(h_mean[:], h_sums[:], AX.X, ALU.add))
                nc.vector.tensor_scalar(mean_lhs[:], ones, h_mean[:], 1.0 / N, ALU.mult, ALU.mult
                                        ).then_inc(h_mean_ready, 1)
                link(nc.vector.tensor_scalar(scale_a[:], scale_a[:], one_col[:, 11:12], None, ALU.mult))
                nc.vector.tensor_scalar(scale_a_lo[:], scale_a[:], 1.0 / LO, None, ALU.mult)
                link(nc.vector.tensor_scalar(scale_c[:], cols[:, 5, :], one_col[:, 3:4], exp(slope * SHIFT) / TOP,
                                             ALU.mult, ALU.mult))
                nc.vector.tensor_scalar(scale_c_lo[:], scale_c[:], 1.0 / LO, None, ALU.mult)
                v = shallow_values[:, :, :, F]
                link(nc.vector.tensor_copy(v[:, :, 0], shallow_f))
                link(nc.vector.tensor_tensor(rest, shallow_f, v[:, :, 0], ALU.subtract))
                nc.vector.tensor_scalar(v[:, :, 1], rest, LO, None, ALU.mult)
                dve.wait_ge(mean_done, l + 1)
                nc.vector.tensor_copy(mean_wh[:], acc[1][:, 0:F])
                def masks(k, *chunks):
                    if l == 1:
                        return
                    for c in chunks:
                        n = k * CHUNKS + c
                        loads = CHUNKS // ADJ_SLOTS * k + c // ADJ_SLOTS + 1
                        dve.wait_ge(adj_loaded[c % ADJ_SLOTS], 16 * loads)
                        if not (isinstance(k, int) and n < MASK_SLOTS):
                            dve.wait_ge(chunk_packed, n - (MASK_SLOTS - 1))
                        dve.nop(nofuse=True)
                        nc.vector.tensor_scalar(mask[:, c % MASK_SLOTS, :], adj_in[:, c % ADJ_SLOTS, :], 0.0, None,
                                                ALU.is_gt, saturate=False).then_inc(mask_ready, 1)

                masks(0, *range(HALF_CHUNKS))

                def cut_values(narrow):
                    steep = steep_narrow if narrow else steep_wide
                    dve.wait_ge(steep_cut, 2 * l + 1)
                    nc.vector.tensor_tensor(hs, hs, steep[:, :, 0, 0:F], ALU.subtract).then_inc(scaled, 1)
                    dve.wait_ge(shallow_cut, 2 * l + 1)
                    nc.vector.tensor_tensor(ts, ts, shallow_values[:, :, 0, 0:F], ALU.subtract).then_inc(scaled, 1)
                    v, rest = steep[:, :, :, F], cols[:, 7, :]
                    by = 2 if narrow else 1
                    link(nc.vector.tensor_copy(v[:, :, 0], steep_f), by)
                    link(nc.vector.tensor_tensor(rest, steep_f, v[:, :, 0], ALU.subtract), by)
                    if not narrow:
                        link(nc.vector.tensor_copy(v[:, :, 1], rest))
                        link(nc.vector.tensor_tensor(v[:, :, 2], rest, v[:, :, 1], ALU.subtract))
                    dve.wait_ge(scaled, 4 * l + 4)
                    nc.vector.tensor_scalar(shallow_values[:, :, 1, 0:F], ts, LO, None, ALU.mult
                                            ).then_inc(shallow_cut, 1)
                    dve.wait_ge(steep_cut, 2 * l + 2)
                    if narrow:
                        last = nc.vector.tensor_scalar(v[:, :, 1], rest, LO, None, ALU.mult)
                    else:
                        last = nc.vector.tensor_tensor(steep[:, :, 2, 0:F], hs, steep[:, :, 1, 0:F], ALU.subtract)
                    last.then_inc(values_ready, 1)

                dve.wait_ge(flag_ready, l + 1)
                is_narrow = dve.value_load(flag[0:1, l:l + 1])
                before = done[0]
                with dve.If(is_narrow == 1):
                    cut_values(True)
                done[0] = before
                with dve.Else():
                    cut_values(False)

                def read_words(k, half):
                    if l == 0 and half == 0:
                        return
                    n = l * TILES + k
                    dve.wait_ge(chunk_packed, n * CHUNKS + (half + 1) * HALF_CHUNKS)
                    if l == 0:
                        nc.vector.tensor_copy(packed[:, bass.ds(k * TW + half * HW, HW)], pack[half][:, 0, :])
                    if not (l == 0 and isinstance(k, int) and k == 0):
                        dve.wait_ge(split_step, 2 * n)
                    nc.vector.tensor_scalar(sign_words[:, half * HW:(half + 1) * HW], pack[half][:, 1, :],
                                            float(2 ** BITS - 1), 0.5, ALU.add, ALU.mult).then_inc(words_read[half], 1)

                def split_words(k):
                    n = l * TILES + k
                    if not (l == 0 and isinstance(k, int) and k == 0):
                        for w in range(2):
                            dve.wait_ge(mat_ready[w], n)
                    for half in range(2):
                        dve.wait_ge(words_read[half], n + 1)
                    here = packed[:, bass.ds(k * TW, TW)]
                    nc.vector.tensor_tensor(steep_words[:], here, sign_words[:], ALU.bitwise_and
                                            ).then_inc(split_step, 1)
                    dve.wait_ge(split_step, 2 * n + 1)
                    nc.vector.tensor_tensor(shallow_words[:], here, steep_words[:], ALU.bitwise_xor
                                            ).then_inc(split_step, 1)

                def unpack(k, w):
                    n = l * TILES + k
                    if not (l == 0 and isinstance(k, int) and k == 0):
                        dve.wait_ge(mat_used[w], n)
                    dve.wait_ge(split_step, 2 * n + 1 + w)
                    words = (steep_words, shallow_words)[w][:].rearrange("p (b g) -> p b g", b=BLOCKS)
                    to = work[:, w].bitcast(U16)
                    for b in range(BITS // 2):
                        if b <= 6:
                            shift, op = 6 - b, ALU.logical_shift_left
                        else:
                            shift, op = b - 6, ALU.logical_shift_right
                        ins = nc.vector.tensor_scalar(to[:, :, b * WORDS:(b + 1) * WORDS], words, shift,
                                                      TWO_TWICE, op, ALU.bitwise_and)
                    ins.then_inc(mat_ready[w], 1)

                def shallow_sums(k):
                    if l == 0:
                        return
                    n = l * TILES + k
                    dve.wait_ge(mat_used[1], n + 1)
                    dve.wait_ge(sums_used, n)
                    dve.nop(nofuse=True)
                    nc.vector.tensor_scalar(sums[:, 0, :], acc[1][:, 0:C1], scale_c[:, bass.ds(k, 1)], None, ALU.mult)
                    nc.vector.tensor_scalar(sums[:, 1, :], acc[1][:, C1:2 * C1], scale_c_lo[:, bass.ds(k, 1)], None,
                                            ALU.mult).then_inc(sums_ready[1], 1)

                def epilogue(k, narrow):
                    n = l * TILES + k
                    at = [0]

                    def then(ins):
                        at[0] += 1
                        ins.then_inc(epi, 1)
                        dve.wait_ge(epi, n * EPI_STEPS + at[0])

                    if not (l == 0 and isinstance(k, int) and k == 0):
                        dve.wait_ge(epi, n * EPI_STEPS)
                        dve.wait_ge(out_ready, n)
                    dve.wait_ge(sums_ready[0], n + 1)
                    dve.wait_ge(sums_ready[1], n + 1)
                    parts = PARTS + (PARTS if narrow else WIDE_PARTS)
                    ins = nc.vector.tensor_reduce(total[:], sums[:, 0:parts, :].rearrange("p t c -> p c t"),
                                                  AX.X, ALU.add)
                    ins.then_inc(sums_used, 1)
                    dve.wait_ge(sums_used, n + 1)
                    den, empty, full, inv = total[:, F:F + 1], e_small[:, 0:1], e_small[:, 1:2], e_small[:, 2:3]
                    then(nc.vector.tensor_scalar(empty, den, 0.0, None, ALU.is_equal))
                    then(nc.vector.tensor_tensor(full, den, empty, ALU.add))
                    then(nc.vector.reciprocal(inv, full))
                    then(nc.vector.tensor_scalar(e_mid[:, 0, :], total[:, 0:F], inv, None, ALU.mult))
                    then(nc.vector.scalar_tensor_tensor(e_mid[:, 0, :], mean_wh[:], empty, e_mid[:, 0, :],
                                                        ALU.mult, ALU.add))

                def tile(k, narrow, first=False, next1=True, next2=True):
                    H = HALF_CHUNKS
                    if not first:
                        shallow_sums(k - 1)
                    if next1:
                        masks(k + 1, H, H + 1)
                    unpack(k, 1)
                    if next1:
                        read_words(k + 1, 0)
                        masks(k + 1, H + 2)
                    if not first:
                        epilogue(k - 1, narrow)
                    if next1:
                        masks(k + 1, H + 3)
                    if next2:
                        masks(k + 2, 0, 1, 2)
                    if next1:
                        read_words(k + 1, 1)
                        split_words(k + 1)
                        unpack(k + 1, 0)
                    if next2:
                        masks(k + 2, 3)

                dve.wait_ge(thr_stored, 16 * (l + 1))
                dve.wait_ge(values_ready, l + 1)
                masks(0, *range(HALF_CHUNKS, CHUNKS))
                read_words(0, 0)
                masks(1, 0, 1, 2)
                read_words(0, 1)
                split_words(0)
                unpack(0, 0)
                masks(1, 3)

                def tiles(narrow):
                    tile(0, narrow, first=True)
                    with dve.Fori(1, TILES - 2) as k:
                        tile(k, narrow)
                    tile(TILES - 2, narrow, next2=False)
                    tile(TILES - 1, narrow, next1=False, next2=False)

                with dve.If(is_narrow == 1):
                    tiles(True)
                with dve.Else():
                    tiles(False)
                if l == 0:
                    dve.wait_ge(chunk_packed, CHUNKS * TILES)
                    centre(1, 0)
                    centre(1, 1)
                shallow_sums(TILES - 1)
                with dve.If(is_narrow == 1):
                    epilogue(TILES - 1, True)
                with dve.Else():
                    epilogue(TILES - 1, False)


_INS = ["x", "adj", "L0_gnn_W", "L0_gnn_a", "L1_gnn_W", "L1_gnn_a"]


def kernel(**inputs):
    import concourse.bacc as _bacc
    from concourse import mybir as _mybir
    from concourse.bass_utils import run_bass_kernel_spmd as _run

    nc = _bacc.Bacc("TRN2", target_bir_lowering=False, num_devices=1)
    given = {name: np.ascontiguousarray(inputs[name]) for name in _INS}
    rows = np.arange(P)
    given["identity"] = np.eye(P, dtype=np.float32)
    given["powers"] = np.where((rows[:, None] % BITS) // 2 == np.arange(WORDS)[None, :],
                               2.0 ** (8 * (rows[:, None] % 2) + rows[:, None] // BITS), 0.0).astype(np.float32)
    arrays, args = {}, []
    for name, a in given.items():
        arrays[f"in_{name}"] = a
        args.append(nc.dram_tensor(f"in_{name}", a.shape, _mybir.dt.from_np(a.dtype), kind="ExternalInput").ap())
    n, f = given["x"].shape
    args.append(nc.dram_tensor("out_x", (n, f), _mybir.dt.float32, kind="ExternalOutput").ap())
    two_layer_graph_attention(nc, *args)
    r = _run(nc, [arrays], core_ids=[0])
    return r.results[0]["out_x"]
```
